# Optimizing a Trainium2 kernel written in Bass

```python
import numpy as np
import jax
import jax.numpy as jnp

def _softmax(x, axis=-1):
    return jax.nn.softmax(x, axis=axis)

def _gelu(x):
    return jax.nn.gelu(x, approximate=True)

def _silu(x):
    return jax.nn.silu(x)

def _sigmoid(x):
    return jax.nn.sigmoid(x)

def _layernorm(x, axis=-1, eps=1e-05):
    m = jnp.mean(x, axis=axis, keepdims=True)
    v = jnp.var(x, axis=axis, keepdims=True)
    return (x - m) / jnp.sqrt(v + eps)

def _scatter_add(tgt, idx, src, axis=0):
    return tgt.at[idx].add(src)

def _segment_sum(src, seg, n):
    return jax.ops.segment_sum(src, seg, n)
kernel_name = 'mk_gnn_ffn_d1_gnn_r8_17f448'

def setup_inputs(seed: int=0):
    np.random.seed(seed)
    _w = jnp.asarray

    def _rec_inputs():
        import jax
        import jax.numpy as jnp
        _gk = jax.random.key(seed)
        x = -0.0003713 + 1 * jax.random.normal(jax.random.fold_in(_gk, 1), (6250, 256), jnp.float32)
        _s = jax.random.randint(jax.random.fold_in(_gk, 2), (100000,), 0, 6250, jnp.int32)
        _d = jax.random.randint(jax.random.fold_in(_gk, 3), (100000,), 0, 6250, jnp.int32)
        _loop = jnp.arange(6250, dtype=jnp.int32)
        src = jnp.concatenate([_s, _d, _loop])
        dst = jnp.concatenate([_d, _s, _loop])
        _o = jnp.argsort(dst, stable=True)
        src = src[_o]
        dst = dst[_o]
        edge_attr_64 = 0.000189758 + 1.00013 * jax.random.normal(jax.random.fold_in(_gk, 11), (206250, 64), jnp.float32)
        return (x, src, dst, edge_attr_64)
    x, src, dst, edge_attr_64 = _rec_inputs()

    def _L0_gnn_setup():
        import jax, jax.numpy as jnp
        import numpy as np
        N, E, HID, HEADS, EDIM = (6250, 100000, 256, 8, 64)
        C = HID // HEADS

        def _layernorm(x, g, b, eps=1e-05):
            mu = jnp.mean(x, axis=-1, keepdims=True)
            var = jnp.var(x, axis=-1, keepdims=True)
            return (x - mu) * jax.lax.rsqrt(var + eps) * g + b

        def _transformer_conv(x, edge_index, edge_attr, Wq, bq, Wk, bk, Wv, bv, We, Wskip, bskip, Wbeta):
            n = x.shape[0]
            src, dst = (edge_index[0], edge_index[1])
            q = (x @ Wq.T + bq).reshape(n, HEADS, C)
            k = (x @ Wk.T + bk).reshape(n, HEADS, C)
            v = (x @ Wv.T + bv).reshape(n, HEADS, C)
            e = (edge_attr @ We.T).reshape(-1, HEADS, C)
            k_e = k[src] + e
            v_e = v[src] + e
            alpha = jnp.sum(q[dst] * k_e, axis=-1) / np.sqrt(C)
            amax = jax.ops.segment_max(alpha, dst, num_segments=n)
            amax = jnp.where(jnp.isfinite(amax), amax, 0.0)
            ex = jnp.exp(alpha - amax[dst])
            denom = jax.ops.segment_sum(ex, dst, num_segments=n)
            alpha = ex / (denom[dst] + 1e-16)
            out = jax.ops.segment_sum(v_e * alpha[..., None], dst, num_segments=n)
            out = out.reshape(n, HEADS * C)
            x_r = x @ Wskip.T + bskip
            beta = jax.nn.sigmoid(jnp.concatenate([out, x_r, out - x_r], axis=-1) @ Wbeta.T)
            return beta * x_r + (1.0 - beta) * out
        key = jax.random.key(seed)
        ks = jax.random.split(key, 20)
        s_in = 1.0 / np.sqrt(HID)
        s_e = 1.0 / np.sqrt(EDIM)
        s_ff = 1.0 / np.sqrt(4 * HID)
        s_b = 1.0 / np.sqrt(3 * HID)
        return {'x': jax.random.normal(ks[0], (N, HID), jnp.float32), 'edge_index': jax.random.randint(ks[1], (2, E), 0, N, jnp.int32), 'edge_attr': jax.random.normal(ks[2], (E, EDIM), jnp.float32), 'Wq': jax.random.uniform(ks[3], (HID, HID), jnp.float32, -s_in, s_in), 'bq': jnp.zeros((HID,), jnp.float32), 'Wk': jax.random.uniform(ks[4], (HID, HID), jnp.float32, -s_in, s_in), 'bk': jnp.zeros((HID,), jnp.float32), 'Wv': jax.random.uniform(ks[5], (HID, HID), jnp.float32, -s_in, s_in), 'bv': jnp.zeros((HID,), jnp.float32), 'We': jax.random.uniform(ks[6], (HID, EDIM), jnp.float32, -s_e, s_e), 'Wskip': jax.random.uniform(ks[7], (HID, HID), jnp.float32, -s_in, s_in), 'bskip': jnp.zeros((HID,), jnp.float32), 'Wbeta': jax.random.uniform(ks[8], (1, 3 * HID), jnp.float32, -s_b, s_b), 'ln1_g': jnp.ones((HID,), jnp.float32), 'ln1_b': jnp.zeros((HID,), jnp.float32), 'ln2_g': jnp.ones((HID,), jnp.float32), 'ln2_b': jnp.zeros((HID,), jnp.float32), 'W1': jax.random.uniform(ks[9], (4 * HID, HID), jnp.float32, -s_in, s_in), 'b1': jnp.zeros((4 * HID,), jnp.float32), 'W2': jax.random.uniform(ks[10], (HID, 4 * HID), jnp.float32, -s_ff, s_ff), 'b2': jnp.zeros((HID,), jnp.float32)}
    _L0_gnn_all = _L0_gnn_setup()
    _L0_gnn_in = {k: v for k, v in _L0_gnn_all.items() if k in ('Wq', 'bq', 'Wk', 'bk', 'Wv', 'bv', 'We', 'Wskip', 'bskip', 'Wbeta', 'ln1_g', 'ln1_b', 'ln2_g', 'ln2_b', 'W1', 'b1', 'W2', 'b2')}
    del _L0_gnn_all

    def _L0_ffn_setup():
        import jax, jax.numpy as jnp
        import numpy as np
        B, A = (512, 8)
        IN, OUT = (256, 256)
        SH1, SH2 = (256, 128)
        EH1, EH2 = (128, 64)
        E, TOPK = (4, 2)

        def _shared_mlp(x, W1, b1, W2, b2, W3, b3):
            h = jax.nn.relu(x @ W1 + b1)
            h = jax.nn.relu(h @ W2 + b2)
            return h @ W3 + b3

        def _experts_mlp(x, eW1, eb1, eW2, eb2, eW3, eb3):
            h = jax.nn.relu(jnp.einsum('baf,efh->ebah', x, eW1) + eb1[:, None, None, :])
            h = jax.nn.relu(jnp.einsum('ebah,ehg->ebag', h, eW2) + eb2[:, None, None, :])
            o = jnp.einsum('ebag,ego->ebao', h, eW3) + eb3[:, None, None, :]
            return jnp.moveaxis(o, 0, -1)
        key = jax.random.key(seed)
        ks = jax.random.split(key, 16)
        s = 0.05
        return {'x': jax.random.normal(ks[0], (B, A, IN), jnp.float32), 'sW1': jax.random.normal(ks[1], (IN, SH1), jnp.float32) * s, 'sb1': jnp.zeros((SH1,), jnp.float32), 'sW2': jax.random.normal(ks[2], (SH1, SH2), jnp.float32) * s, 'sb2': jnp.zeros((SH2,), jnp.float32), 'sW3': jax.random.normal(ks[3], (SH2, OUT), jnp.float32) * s, 'sb3': jnp.zeros((OUT,), jnp.float32), 'eW1': jax.random.normal(ks[4], (E, IN, EH1), jnp.float32) * s, 'eb1': jnp.zeros((E, EH1), jnp.float32), 'eW2': jax.random.normal(ks[5], (E, EH1, EH2), jnp.float32) * s, 'eb2': jnp.zeros((E, EH2), jnp.float32), 'eW3': jax.random.normal(ks[6], (E, EH2, OUT), jnp.float32) * s, 'eb3': jnp.zeros((E, OUT), jnp.float32), 'gW': jax.random.normal(ks[7], (IN, E), jnp.float32) * s, 'gb': jnp.zeros((E,), jnp.float32)}
    _L0_ffn_all = _L0_ffn_setup()
    _L0_ffn_in = {k: v for k, v in _L0_ffn_all.items() if k in ('sW1', 'sb1', 'sW2', 'sb2', 'sW3', 'sb3', 'eW1', 'eb1', 'eW2', 'eb2', 'eW3', 'eb3', 'gW', 'gb')}
    del _L0_ffn_all
    return {'x': x, 'src': src, 'dst': dst, 'edge_attr_64': edge_attr_64, 'L0_gnn_Wq': _L0_gnn_in['Wq'], 'L0_gnn_bq': _L0_gnn_in['bq'], 'L0_gnn_Wk': _L0_gnn_in['Wk'], 'L0_gnn_bk': _L0_gnn_in['bk'], 'L0_gnn_Wv': _L0_gnn_in['Wv'], 'L0_gnn_bv': _L0_gnn_in['bv'], 'L0_gnn_We': _L0_gnn_in['We'], 'L0_gnn_Wskip': _L0_gnn_in['Wskip'], 'L0_gnn_bskip': _L0_gnn_in['bskip'], 'L0_gnn_Wbeta': _L0_gnn_in['Wbeta'], 'L0_gnn_ln1_g': _L0_gnn_in['ln1_g'], 'L0_gnn_ln1_b': _L0_gnn_in['ln1_b'], 'L0_gnn_ln2_g': _L0_gnn_in['ln2_g'], 'L0_gnn_ln2_b': _L0_gnn_in['ln2_b'], 'L0_gnn_W1': _L0_gnn_in['W1'], 'L0_gnn_b1': _L0_gnn_in['b1'], 'L0_gnn_W2': _L0_gnn_in['W2'], 'L0_gnn_b2': _L0_gnn_in['b2'], 'L0_ffn_sW1': _L0_ffn_in['sW1'], 'L0_ffn_sb1': _L0_ffn_in['sb1'], 'L0_ffn_sW2': _L0_ffn_in['sW2'], 'L0_ffn_sb2': _L0_ffn_in['sb2'], 'L0_ffn_sW3': _L0_ffn_in['sW3'], 'L0_ffn_sb3': _L0_ffn_in['sb3'], 'L0_ffn_eW1': _L0_ffn_in['eW1'], 'L0_ffn_eb1': _L0_ffn_in['eb1'], 'L0_ffn_eW2': _L0_ffn_in['eW2'], 'L0_ffn_eb2': _L0_ffn_in['eb2'], 'L0_ffn_eW3': _L0_ffn_in['eW3'], 'L0_ffn_eb3': _L0_ffn_in['eb3'], 'L0_ffn_gW': _L0_ffn_in['gW'], 'L0_ffn_gb': _L0_ffn_in['gb']}

def reference(x, src, dst, edge_attr_64, L0_gnn_Wq, L0_gnn_bq, L0_gnn_Wk, L0_gnn_bk, L0_gnn_Wv, L0_gnn_bv, L0_gnn_We, L0_gnn_Wskip, L0_gnn_bskip, L0_gnn_Wbeta, L0_gnn_ln1_g, L0_gnn_ln1_b, L0_gnn_ln2_g, L0_gnn_ln2_b, L0_gnn_W1, L0_gnn_b1, L0_gnn_W2, L0_gnn_b2, L0_ffn_sW1, L0_ffn_sb1, L0_ffn_sW2, L0_ffn_sb2, L0_ffn_sW3, L0_ffn_sb3, L0_ffn_eW1, L0_ffn_eb1, L0_ffn_eW2, L0_ffn_eb2, L0_ffn_eW3, L0_ffn_eb3, L0_ffn_gW, L0_ffn_gb):
    import jax
    import jax.numpy as jnp

    def _L0_gnn_ref(x, edge_index, edge_attr, Wq, bq, Wk, bk, Wv, bv, We, Wskip, bskip, Wbeta, ln1_g, ln1_b, ln2_g, ln2_b, W1, b1, W2, b2):
        import jax, jax.numpy as jnp
        import numpy as np
        N, E, HID, HEADS, EDIM = (6250, 100000, 256, 8, 64)
        C = HID // HEADS

        def _layernorm(x, g, b, eps=1e-05):
            mu = jnp.mean(x, axis=-1, keepdims=True)
            var = jnp.var(x, axis=-1, keepdims=True)
            return (x - mu) * jax.lax.rsqrt(var + eps) * g + b

        def _transformer_conv(x, edge_index, edge_attr, Wq, bq, Wk, bk, Wv, bv, We, Wskip, bskip, Wbeta):
            n = x.shape[0]
            src, dst = (edge_index[0], edge_index[1])
            q = (x @ Wq.T + bq).reshape(n, HEADS, C)
            k = (x @ Wk.T + bk).reshape(n, HEADS, C)
            v = (x @ Wv.T + bv).reshape(n, HEADS, C)
            e = (edge_attr @ We.T).reshape(-1, HEADS, C)
            k_e = k[src] + e
            v_e = v[src] + e
            alpha = jnp.sum(q[dst] * k_e, axis=-1) / np.sqrt(C)
            amax = jax.ops.segment_max(alpha, dst, num_segments=n)
            amax = jnp.where(jnp.isfinite(amax), amax, 0.0)
            ex = jnp.exp(alpha - amax[dst])
            denom = jax.ops.segment_sum(ex, dst, num_segments=n)
            alpha = ex / (denom[dst] + 1e-16)
            out = jax.ops.segment_sum(v_e * alpha[..., None], dst, num_segments=n)
            out = out.reshape(n, HEADS * C)
            x_r = x @ Wskip.T + bskip
            beta = jax.nn.sigmoid(jnp.concatenate([out, x_r, out - x_r], axis=-1) @ Wbeta.T)
            return beta * x_r + (1.0 - beta) * out
        h = _transformer_conv(x, edge_index, edge_attr, Wq, bq, Wk, bk, Wv, bv, We, Wskip, bskip, Wbeta)
        x = _layernorm(x + h, ln1_g, ln1_b)
        h = jax.nn.gelu(x @ W1.T + b1, approximate=False) @ W2.T + b2
        return _layernorm(x + h, ln2_g, ln2_b)

    def _L0_ffn_ref(x, sW1, sb1, sW2, sb2, sW3, sb3, eW1, eb1, eW2, eb2, eW3, eb3, gW, gb):
        import jax, jax.numpy as jnp
        import numpy as np
        B, A = (512, 8)
        IN, OUT = (256, 256)
        SH1, SH2 = (256, 128)
        EH1, EH2 = (128, 64)
        E, TOPK = (4, 2)

        def _shared_mlp(x, W1, b1, W2, b2, W3, b3):
            h = jax.nn.relu(x @ W1 + b1)
            h = jax.nn.relu(h @ W2 + b2)
            return h @ W3 + b3

        def _experts_mlp(x, eW1, eb1, eW2, eb2, eW3, eb3):
            h = jax.nn.relu(jnp.einsum('baf,efh->ebah', x, eW1) + eb1[:, None, None, :])
            h = jax.nn.relu(jnp.einsum('ebah,ehg->ebag', h, eW2) + eb2[:, None, None, :])
            o = jnp.einsum('ebag,ego->ebao', h, eW3) + eb3[:, None, None, :]
            return jnp.moveaxis(o, 0, -1)
        all_out = _experts_mlp(x, eW1, eb1, eW2, eb2, eW3, eb3)
        shared = _shared_mlp(x, sW1, sb1, sW2, sb2, sW3, sb3)
        gates = jax.nn.softmax(x @ gW + gb, axis=-1)
        topv, topi = jax.lax.top_k(gates, TOPK)
        topw = jax.nn.softmax(topv, axis=-1)
        sel = jnp.take_along_axis(all_out, topi[:, :, None, :], axis=-1)
        gated = jnp.sum(sel * topw[:, :, None, :], axis=-1)
        return shared + gated
    edge_index = jnp.stack([src, dst])
    x = x + _L0_gnn_ref(_layernorm(x, axis=-1), edge_index, edge_attr_64, L0_gnn_Wq, L0_gnn_bq, L0_gnn_Wk, L0_gnn_bk, L0_gnn_Wv, L0_gnn_bv, L0_gnn_We, L0_gnn_Wskip, L0_gnn_bskip, L0_gnn_Wbeta, L0_gnn_ln1_g, L0_gnn_ln1_b, L0_gnn_ln2_g, L0_gnn_ln2_b, L0_gnn_W1, L0_gnn_b1, L0_gnn_W2, L0_gnn_b2)
    x = x + _L0_ffn_ref(_layernorm(x, axis=-1)[None], L0_ffn_sW1, L0_ffn_sb1, L0_ffn_sW2, L0_ffn_sb2, L0_ffn_sW3, L0_ffn_sb3, L0_ffn_eW1, L0_ffn_eb1, L0_ffn_eW2, L0_ffn_eb2, L0_ffn_eW3, L0_ffn_eb3, L0_ffn_gW, L0_ffn_gb)[0]
    return x

_drawn_inputs = setup_inputs


def setup_inputs(seed=0):
    import zlib

    import numpy as np

    out = dict(_drawn_inputs(seed))
    spreads = {'L0_gnn_bq': (0.0, 0.8),
     'L0_gnn_bk': (0.0, 2.0),
     'L0_gnn_bv': (0.0, 0.276),
     'L0_gnn_bskip': (0.0, 0.317),
     'L0_gnn_ln1_g': (1.0, 0.2),
     'L0_gnn_ln1_b': (0.0, 0.1),
     'L0_gnn_ln2_g': (1.0, 0.2),
     'L0_gnn_ln2_b': (0.0, 0.1),
     'L0_gnn_b1': (0.0, 0.463),
     'L0_gnn_b2': (0.0, 0.1),
     'L0_ffn_sb1': (0.0, 0.772),
     'L0_ffn_sb2': (0.0, 0.373),
     'L0_ffn_sb3': (0.0, 0.1),
     'L0_ffn_eb1': (0.0, 2.0),
     'L0_ffn_eb2': (0.0, 0.8),
     'L0_ffn_eb3': (0.0, 0.1),
     'L0_ffn_gb': (0.0, 0.687)}
    factors = {'L0_gnn_Wk': 3.831}
    for name, (base, spread) in spreads.items():
        noise = np.random.default_rng([zlib.crc32(name.encode()), seed]).standard_normal(out[name].shape)
        drawn = base * np.exp(spread * noise) if base else spread * noise
        out[name] = jnp.asarray(drawn.astype(out[name].dtype))
    for name, factor in factors.items():
        out[name] = (out[name] * factor).astype(out[name].dtype)
    return out
```

```python
from contextlib import ExitStack

import numpy as np
import concourse.bass as bass
from concourse import mybir

F32 = mybir.dt.float32
I32 = mybir.dt.int32
U32 = mybir.dt.uint32
ALU = mybir.AluOpType
ACT = mybir.ActivationFunctionType
AX = mybir.AxisListType

P = 128
BIG = 1.0e30
FLOOR = 1.0e29
LN_EPS = 1e-5


def mean_and_var(dve, ch, stats, mean, var, n):
    ch.step(dve.tensor_tensor(mean[:, :], stats[:, :, 1], stats[:, :, 4], ALU.subtract))
    ch.step(dve.tensor_tensor(var[:, :], mean[:, :], mean[:, :], ALU.mult))
    ch.step(dve.scalar_tensor_tensor(out=var[:, :], in0=var[:, :], scalar=n / 4.0, in1=stats[:, :, 2], op0=ALU.mult, op1=ALU.add))
    ch.step(dve.tensor_tensor(var[:, :], var[:, :], stats[:, :, 5], ALU.add))
    ch.step(dve.tensor_scalar(var[:, :], var[:, :], 1.0 / n, None, ALU.mult))
    ch.step(dve.tensor_tensor(mean[:, :], stats[:, :, 1], stats[:, :, 4], ALU.add))
    ch.step(dve.tensor_scalar(mean[:, :], mean[:, :], 0.5, None, ALU.mult))


def build(nc, a, out):
    N = out.shape[0]
    D = a["x"].shape[1]
    NP = a["x"].shape[0]
    NB = NP // P
    H = 8
    C = D // H
    DE = a["edge_attr"].shape[1]
    GN = P // H
    GB = P // GN
    NG = NB * GB
    T = a["tiles"]
    CH = T * P
    E = a["edges"]
    NCH = a["dst"].shape[0] // P
    KD = D // P
    FW = 3 * P
    ONE = D + DE
    NEQ = ONE + 1
    K3 = DE + 1 + GN
    ZW = D + DE + 1
    CW = C + 1
    SCALE = 1.0 / float(np.sqrt(C))
    SLOTS = 4
    W7 = 7 if NB % 7 == 0 else 1
    N7 = NB // W7
    HID = a["W1T"].shape[1]
    KH = HID // P
    NE = a["gW"].shape[1]
    EH2 = a["eW2"].shape[2]
    BC = -(-(NG + 1) // P)

    xn_d = nc.dram_tensor("xn_rows", [NP, D], F32, kind="Internal").ap()
    bound_d = nc.dram_tensor("bounds", [BC * P], I32, kind="Internal").ap()
    x_d = a["x"].rearrange("(b p) d -> p b d", p=P)
    xn_v = xn_d.rearrange("(b p) d -> p b d", p=P)
    dst_rows = a["dst"].rearrange("(r c) -> r c", c=P)

    top = ExitStack()

    def sem(name):
        return top.enter_context(nc.semaphore(name))

    class Chain:

        def __init__(self, eng, name):
            self.eng, self.sem, self.n, self.base = eng, sem(name), 0, 0

        def step(self, ins):
            self.n += 1
            ins.then_inc(self.sem, 1)
            self.eng.wait_ge(self.sem, self.base + self.n)

    with top:
        def sbt(stack, name, shape, dt=F32):
            return stack.enter_context(nc.sbuf_tensor(name, shape, dt))

        def pst(stack, name, shape, dt=F32):
            return stack.enter_context(nc.psum_tensor(name, shape, dt))

        ident = sbt(top, "ident", [P, P])
        onesrow = sbt(top, "onesrow", [1, P])
        U = sbt(top, "U", [P, NB, H * CW])
        passes = sbt(top, "passes", [1, 1], I32)
        offs = sbt(top, "offs", [1, NG], I32)

        consts_ready = sem("consts_ready")

        mid = ExitStack()
        with mid:
            qT = sbt(mid, "qT", [P, KD, NP + P])
            with ExitStack() as s1:
                x_all = sbt(s1, "x_all", [P, NB, D])
                xs = sbt(s1, "xs", [P, W7, D])
                xT = sbt(s1, "xT", [P, KD, W7 * P])
                stats = sbt(s1, "stats", [P, NB, 6])
                mean = sbt(s1, "mean", [P, NB])
                var = sbt(s1, "var", [P, NB])
                lnv = sbt(s1, "lnv", [P, NB])
                rstd = sbt(s1, "rstd", [P, NB])
                epsc = sbt(s1, "epsc", [P, 1])
                WqT = sbt(s1, "WqT", [P, KD, D])
                bq = sbt(s1, "bq", [P, KD])
                bqs = sbt(s1, "bqs", [P, KD])
                firsts = sbt(s1, "firsts", [P, NCH], I32)
                hits = sbt(s1, "hits", [P, NCH])
                hits2 = sbt(s1, "hits2", [P, P])
                bval = sbt(s1, "bval", [P, BC])
                cnt = sbt(s1, "cnt", [P, BC])
                rowi = sbt(s1, "rowi", [P, BC], I32)
                drow = sbt(s1, "drow", [P, BC, P], I32)
                cnt2 = sbt(s1, "cnt2", [P, BC])
                starti = sbt(s1, "starti", [P, BC], I32)
                srow = sbt(s1, "srow", [1, BC * P], I32)
                srowf = sbt(s1, "srowf", [1, BC * P])
                lens = sbt(s1, "lens", [1, NG])
                mlen = sbt(s1, "mlen", [1, 1])
                tp = [pst(s1, f"tp{i}", [P, KD, P]) for i in range(2)]
                pq = [pst(s1, f"pq{i}", [P, 4 * P]) for i in range(2)]

                x_landed, w_landed, first_landed = sem("x_landed"), sem("w_landed"), sem("first_landed")
                rows_gathered, bounds_stored, bounds_landed = sem("rows_g"), sem("bounds_stored"), sem("bounds_landed")
                tiles_seen = sem("tiles_seen")
                stats_done, rstd_done, xn_ready, xn_stored = sem("stats_done"), sem("rstd_done"), sem("xn_ready"), sem("xn_st")
                tp_filled, tp_emptied, q_filled, q_emptied = sem("tp_f"), sem("tp_e"), sem("q_f"), sem("q_e")
                bval_ready, rowi_ready, start_ready = sem("bval_r"), sem("rowi_r"), sem("start_r")
                q_steps = [(h0, min(4, W7 - h0)) for h0 in range(0, W7, 4)]
                Q7 = len(q_steps) * KD

                with nc.Block() as block:
                    @block.sync
                    def _(sp):
                        sp.dma_start(firsts[:, :], a["dst_first"].partition_broadcast(P)).then_inc(first_landed, 16)
                        sp.dma_start(x_all[:, :, :], x_d).then_inc(x_landed, 16)
                        sp.dma_start(WqT[:, :, :], a["WqT"].rearrange("(k p) c -> p k c", p=P)).then_inc(w_landed, 16)
                        sp.dma_start(bq[:, :], a["bq"]).then_inc(w_landed, 16)
                        sp.wait_ge(start_ready, 1)
                        sp.dma_start(bound_d.rearrange("(c p) -> p c", p=P), starti[:, :]).then_inc(bounds_stored, 16)
                        sp.wait_ge(bounds_stored, 16)
                        sp.dma_start(srow[:, :], bound_d.rearrange("(a n) -> a n", a=1)).then_inc(bounds_landed, 16)
                        with sp.Fori(0, N7) as i:
                            sp.wait_ge(xn_ready, (i + 1) * W7)
                            sp.dma_start(xn_v[:, bass.ds(i * W7, W7), :], xs[:, :, :]).then_inc(xn_stored, 16)
                        sp.wait_ge(xn_stored, 16 * N7)

                    @block.gpsimd
                    def _(pool):
                        pool.memset(ident[:, :], 0.0).then_inc(consts_ready, 1)
                        pool.memset(onesrow[:, :], 1.0).then_inc(consts_ready, 1)
                        pool.iota(rowi[:, :], pattern=[[GN * P, BC]], base=0, channel_multiplier=GN).then_inc(bval_ready, 1)
                        pool.wait_ge(consts_ready, 2)
                        pool.affine_select(out=ident[:, :], in_=ident[:, :], compare_op=ALU.not_equal, fill=1.0,
                                           base=0, pattern=[[-1, P]], channel_multiplier=1).then_inc(consts_ready, 1)
                        pool.wait_ge(rowi_ready, 1)
                        for c in range(BC):
                            pool.indirect_dma_start(
                                out=drow[:, c, :], out_offset=None, in_=dst_rows,
                                in_offset=bass.IndirectOffsetOnAxis(ap=rowi[:, c:c + 1], axis=0),
                            ).then_inc(rows_gathered, 16)
                        pool.wait_ge(rows_gathered, 16 * BC)

                    @block.vector
                    def _(dve):
                        ch = Chain(dve, "dve1")
                        ch.step(dve.memset(epsc[:, :], LN_EPS))
                        dve.memset(U[:, :, :], 0.0)
                        dve.wait_ge(bval_ready, 1)
                        ch.step(dve.tensor_copy(bval[:, :], rowi[:, :]))
                        dve.wait_ge(first_landed, 16)
                        for c in range(BC):
                            ch.step(dve.tensor_scalar(hits[:, :], firsts[:, :], bval[:, c:c + 1], 0.0, ALU.is_lt, ALU.add,
                                                      accum_out=cnt[:, c:c + 1]))
                        ch.step(dve.tensor_scalar(cnt[:, :], cnt[:, :], -1.0, 0.0, ALU.add, ALU.max))
                        ch.step(dve.tensor_copy(rowi[:, :], cnt[:, :]))
                        dve.sem_inc(rowi_ready, 1)
                        dve.wait_ge(rows_gathered, 16 * BC)
                        for c in range(BC):
                            ch.step(dve.tensor_scalar(hits2[:, :], drow[:, c, :], bval[:, c:c + 1], 0.0, ALU.is_lt, ALU.add,
                                                      accum_out=cnt2[:, c:c + 1]))
                        ch.step(dve.scalar_tensor_tensor(out=cnt[:, :], in0=cnt[:, :], scalar=float(P), in1=cnt2[:, :],
                                                         op0=ALU.mult, op1=ALU.add))
                        dve.tensor_copy(starti[:, :], cnt[:, :]).then_inc(start_ready, 1)
                        dve.wait_ge(bounds_landed, 16)
                        ch.step(dve.tensor_copy(srowf[:, :], srow[:, :]))
                        ch.step(dve.tensor_sub(lens[:, :], srowf[:, 1:NG + 1], srowf[:, 0:NG]))
                        ch.step(dve.tensor_reduce(mlen[:, :], lens[:, :], AX.X, ALU.max))
                        ch.step(dve.tensor_scalar(passes[:, :], mlen[:, :], 1.0, None, ALU.max))
                        ch.step(dve.tensor_scalar(offs[:, :], srowf[:, 0:NG], float(E), None, ALU.min))
                        dve.wait_ge(x_landed, 16)
                        with dve.Fori(0, NB) as i:
                            dve.bn_stats(stats[:, bass.ds(i, 1), :].rearrange("p a d -> p (a d)"),
                                         x_all[:, bass.ds(i, 1), :].rearrange("p a d -> p (a d)")).then_inc(tiles_seen, 1)
                        dve.wait_ge(tiles_seen, NB)
                        mean_and_var(dve, ch, stats, mean, var, D)
                        dve.sem_inc(stats_done, 1)
                        dve.wait_ge(rstd_done, 2)
                        with dve.Fori(0, N7) as i:
                            for j in range(W7):
                                if j == 0:
                                    dve.wait_ge(xn_stored, i * 16)
                                    dve.wait_ge(tp_filled, i * W7)
                                m = i * W7 + j
                                dve.tensor_scalar(xs[:, j, :], x_all[:, bass.ds(m, 1), :].rearrange("p a d -> p (a d)"),
                                                  mean[:, bass.ds(m, 1)],
                                                  rstd[:, bass.ds(m, 1)], ALU.subtract, ALU.mult).then_inc(xn_ready, 1)

                    @block.scalar
                    def _(act):
                        ch = Chain(act, "act1")
                        act.wait_ge(stats_done, 1)
                        act.activation(lnv[:, :], var[:, :], ACT.Ln, bias=epsc[:, 0:1]).then_inc(rstd_done, 1)
                        act.wait_ge(rstd_done, 1)
                        act.activation(rstd[:, :], lnv[:, :], ACT.Exp, scale=-0.5).then_inc(rstd_done, 1)
                        act.wait_ge(w_landed, 32)
                        ch.step(act.mul(bqs[:, :], bq[:, :], SCALE))
                        with act.Fori(0, N7) as i:
                            for j in range(W7):
                                act.wait_ge(tp_filled, i * W7 + j + 1)
                                act.activation(xT[:, :, j * P:(j + 1) * P], tp[(j) % 2][:, :, :], ACT.Copy).then_inc(tp_emptied, 1)
                            for n, (h0, w) in enumerate(q_steps):
                                for c in range(KD):
                                    k = n * KD + c
                                    act.wait_ge(q_filled, i * Q7 + k + 1)
                                    act.activation(qT[:, c, bass.ds((i * W7 + h0) * P, w * P)], pq[k % 2][:, 0:w * P],
                                                   ACT.Identity, bias=bqs[:, c:c + 1], scale=SCALE).then_inc(q_emptied, 1)
                        act.wait_ge(q_emptied, N7 * Q7)
                        act.activation(qT[:, :, NP:NP + P], qT[:, :, 0:P], ACT.Copy)

                    @block.tensor
                    def _(pe):
                        pe.wait_ge(consts_ready, 3)
                        pe.wait_ge(w_landed, 32)
                        with pe.Fori(0, N7) as i:
                            pe.wait_ge(q_emptied, i * Q7)
                            for j in range(W7):
                                pe.wait_ge(xn_ready, i * W7 + j + 1)
                                if j >= 2:
                                    pe.wait_ge(tp_emptied, i * W7 + j - 1)
                                for c in range(KD):
                                    t = pe.transpose(tp[j % 2][:, c, :], xs[:, j, c * P:(c + 1) * P], ident[:, :])
                                t.then_inc(tp_filled, 1)
                            for n, (h0, w) in enumerate(q_steps):
                                pe.wait_ge(tp_emptied, i * W7 + h0 + w)
                                for c in range(KD):
                                    k = n * KD + c
                                    if k >= 2:
                                        pe.wait_ge(q_emptied, i * Q7 + k - 1)
                                    for f in range(KD):
                                        m = pe.matmul(pq[k % 2][:, 0:w * P], WqT[:, f, c * P:(c + 1) * P],
                                                      xT[:, f, h0 * P:(h0 + w) * P], start=(f == 0), stop=(f == KD - 1))
                                    m.then_inc(q_filled, 1)

            with ExitStack() as s2:
                F = [sbt(s2, f"F{i}", [P, T, FW]) for i in range(SLOTS)]
                srci = [sbt(s2, f"srci{i}", [P, T], I32) for i in range(SLOTS)]
                dsti = [sbt(s2, f"dsti{i}", [P, T], I32) for i in range(SLOTS)]
                FT = [sbt(s2, f"FT{i}", [P, 3, CH]) for i in range(2)]
                G = sbt(s2, "G", [P, 3, GB, P])
                Pw = sbt(s2, "Pw", [P, CH])
                PT = sbt(s2, "PT", [P, T, P])
                Zs = sbt(s2, "Zs", [P, FW])
                ZT = sbt(s2, "ZT", [P, 3, H, P])
                nM = sbt(s2, "nM", [P, NB, GB])
                nMo = sbt(s2, "nMo", [P, GB])
                nMn = sbt(s2, "nMn", [P, GB])
                nmx = sbt(s2, "nmx", [P, GB])
                dM = sbt(s2, "dM", [P, GB])
                corr = sbt(s2, "corr", [P, GB])
                cdiag = sbt(s2, "cdiag", [P, GB, GN])
                seln = sbt(s2, "seln", [P, GN])
                selh = sbt(s2, "selh", [P, H])
                nid = sbt(s2, "nid", [P, P])
                Wk = sbt(s2, "Wk", [P, KD, D])
                W3 = sbt(s2, "W3", [P, KD, DE + 1])
                WvT = sbt(s2, "WvT", [P, 3, H, CW])
                Utmp = sbt(s2, "Utmp", [P, H, CW])
                qrow = sbt(s2, "qrow", [P, KD, P])

                ring = [pst(s2, f"ring{i}", [P, 4 * P]) for i in range(2)]
                pS = pst(s2, "pS", [P, 2, 4 * P])
                pPT = [pst(s2, f"pPT{i}", [P, 4 * P]) for i in range(2)]
                pZ = pst(s2, "pZ", [P, 4 * P])
                pM = pst(s2, "pM", [P, 4 * P])

                SH = CH // 2
                TA = (T + 1) // 2
                pt_parts = [(0, TA), (TA, T)]
                HR = P // C
                G_PIECES = [(k, r) for k in range(3) for r in range(HR)]
                NG_P = len(G_PIECES)

                def piece_share(t):
                    return range(t * NG_P // T, (t + 1) * NG_P // T)
                RING = GB * T + NG_P
                assert RING % 2 == 0 and SH <= 512 and GB % SLOTS == 0
                USES = GB // SLOTS

                w2_landed, consts2 = sem("w2_landed"), sem("consts2")
                idx_landed = [sem(f"idx_landed{i}") for i in range(SLOTS)]
                ea_landed = [sem(f"ea_landed{i}") for i in range(SLOTS)]
                gathered = [sem(f"gathered{i}") for i in range(SLOTS)]
                slot_free = sem("slot_free")
                load_turns, gather_turns = sem("load_turns"), sem("gather_turns")
                neq_done, pass_ready, qb_ready = sem("neq_done"), sem("pass_ready"), sem("qb_ready")
                ring_filled, ring_emptied = sem("ring_filled"), sem("ring_emptied")
                s_done, max_done, p_done = sem("s_done"), sem("max_done"), sem("p_done")
                pt_filled, pt_emptied = sem("pt_filled"), sem("pt_emptied")
                z_out, zt_filled, zt_emptied = sem("z_out"), sem("zt_filled"), sem("zt_emptied")
                dM_done, corr_done, cdiag_done, proj_done, merged = (
                    sem("dM_done"), sem("corr_done"), sem("cdiag_done"), sem("proj_done"), sem("merged"))

                NW2 = 7

                def long_loop(eng):
                    longest = eng.value_load(passes[0:1, 0:1], min_val=1, max_val=E)
                    return eng.Fori(0, longest, CH)

                with nc.Block() as block:
                    @block.sync
                    def _(sp):
                        sp.dma_start(Wk[:, :, :], a["Wk"].rearrange("(k p) f -> p k f", p=P)).then_inc(w2_landed, 16)
                        sp.dma_start(W3[:, :, :], a["W3"].rearrange("(k p) f -> p k f", p=P)).then_inc(w2_landed, 16)
                        sp.wait_ge(consts2, 2)
                        for k in range(KD):
                            sp.dma_start(WvT[:, k, :, 0:C], a["WvT"][k * P:(k + 1) * P, :].rearrange("p (h c) -> p h c", h=H)
                                         ).then_inc(w2_landed, 16)
                        sp.dma_start(WvT[0:DE, KD, :, 0:C], a["WeT"].rearrange("p (h c) -> p h c", h=H)).then_inc(w2_landed, 16)
                        sp.dma_start(WvT[DE:DE + 1, KD, :, 0:C], a["bv"].rearrange("(a h c) -> a h c", a=1, h=H)
                                     ).then_inc(w2_landed, 16)
                        sp.dma_start(WvT[DE:DE + 1, KD, :, C:CW], a["ones"].rearrange("(a h c) -> a h c", a=1, h=H)
                                     ).then_inc(w2_landed, 16)
                        with long_loop(sp) as e0:
                            ps = e0 // CH
                            sp.wait_ge(pass_ready, ps + 1)
                            sp.sem_inc(load_turns, 1)
                            with sp.Fori(0, NB) as b:
                                it = sp.snap(ps * NB + b)
                                _, at = nc.values_load_multi_w_load_instructions(
                                    offs[0:1, bass.ds(b * GB, GB)], engines=[mybir.EngineType.SP], min_val=0, max_val=E,
                                    skip_runtime_bounds_check_because="clamped to E by the vector engine")
                                for j in range(GB):
                                    s = j % SLOTS
                                    sp.wait_ge(slot_free, it * GB + (j + 1))
                                    sp.sem_inc(load_turns, 1)
                                    o = at[j]
                                    sp.dma_start(srci[s][:, :], a["src"][bass.ds(o, CH)].rearrange("(p t) -> p t", t=T)
                                                 ).then_inc(idx_landed[s], 16)
                                    sp.dma_start(dsti[s][:, :], a["dst"][bass.ds(o, CH)].rearrange("(p t) -> p t", t=T)
                                                 ).then_inc(idx_landed[s], 16)
                                    sp.dma_start(F[s][:, :, D:D + DE],
                                                 a["edge_attr"][bass.ds(o, CH), :].rearrange("(p t) d -> p t d", t=T)
                                                 ).then_inc(ea_landed[s], 16)

                    @block.gpsimd
                    def _(pool):
                        pool.iota(nid[:, :], pattern=[[1, P]], base=0, channel_multiplier=0,
                                  allow_small_or_imprecise_dtypes=True).then_inc(consts2, 1)
                        pool.memset(WvT[:, :, :, :], 0.0).then_inc(consts2, 1)
                        pool.memset(G[:, KD, :, :], 0.0).then_inc(consts2, 1)
                        pool.memset(seln[:, :], 0.0).then_inc(consts2, 1)
                        pool.memset(selh[:, :], 1.0).then_inc(consts2, 1)
                        pool.wait_ge(consts2, 5)
                        g3 = G[:, KD, :, :].rearrange("p g (h n) -> p (g h) n", n=GN)
                        pool.affine_select(out=g3, in_=g3, compare_op=ALU.not_equal, fill=-BIG, base=-(DE + 1),
                                           pattern=[[0, H * GB], [-1, GN]], channel_multiplier=1).then_inc(consts2, 1)
                        for h in range(H):
                            pool.affine_select(out=seln[:, :], in_=seln[:, :], compare_op=ALU.not_equal, fill=1.0,
                                               base=-GN * h, pattern=[[-1, GN]], channel_multiplier=1).then_inc(consts2, 1)
                            pool.wait_ge(consts2, 7 + h)
                        pool.affine_select(out=selh[:, :], in_=selh[:, :], compare_op=ALU.is_ge, fill=0.0,
                                           base=0, pattern=[[-GN, H]], channel_multiplier=1).then_inc(consts2, 1)
                        pool.wait_ge(consts2, 7 + H)
                        pool.affine_select(out=selh[:, :], in_=selh[:, :], compare_op=ALU.is_ge, fill=0.0,
                                           base=GN - 1, pattern=[[GN, H]], channel_multiplier=-1).then_inc(consts2, 1)
                        with long_loop(pool) as e0:
                            ps = e0 // CH
                            with pool.Fori(0, NB) as b:
                                it = pool.snap(ps * NB + b)
                                for j in range(GB):
                                    s = j % SLOTS
                                    pool.wait_ge(idx_landed[s], it * (32 * USES) + 32 * (j // SLOTS + 1))
                                    pool.sem_inc(gather_turns, 1)
                                    for t in range(T):
                                        pool.indirect_dma_start(
                                            out=F[s][:, t, 0:D], out_offset=None, in_=xn_d,
                                            in_offset=bass.IndirectOffsetOnAxis(ap=srci[s][:, t:t + 1], axis=0),
                                        ).then_inc(gathered[s], 16)

                    CONSTS2 = 8 + H

                    @block.vector
                    def _(dve):
                        ch = Chain(dve, "dve2")
                        for s in range(SLOTS):
                            ch.step(dve.memset(F[s][:, :, ONE:FW], 0.0))
                            dve.memset(F[s][:, :, ONE:ONE + 1], 1.0).then_inc(slot_free, 1)
                        ch.step(dve.memset(Zs[:, :], 0.0))
                        ch.step(dve.memset(nM[:, :, :], FLOOR))
                        dve.wait_ge(consts2, CONSTS2)
                        dve.sem_inc(pass_ready, 1)
                        dve.tensor_copy(qrow[:, :, :], qT[:, :, 0:P]).then_inc(qb_ready, 1)
                        base = ch.n
                        BATCH = GB + 5
                        with long_loop(dve) as e0:
                            ps = e0 // CH
                            pbase = ps * (NB * BATCH + 2)
                            with dve.Fori(0, NB) as b:
                                it = dve.snap(ps * NB + b)
                                ch.base, ch.n = dve.snap(pbase + b * BATCH + base), 0

                                def neq(j):
                                    s = j % SLOTS
                                    dve.wait_ge(idx_landed[s], it * (32 * USES) + 32 * (j // SLOTS + 1))
                                    dve.tensor_tensor(
                                        F[s][:, :, NEQ:NEQ + GN], dsti[s][:, :, None].to_broadcast([P, T, GN]),
                                        nid[:, None, j * GN:(j + 1) * GN].to_broadcast([P, T, GN]),
                                        ALU.not_equal).then_inc(neq_done, 1)

                                def zt_out(j):
                                    dve.wait_ge(zt_filled, it * GB + j + 1)
                                    dve.tensor_copy(
                                        ZT[:, :, :, j * GN:(j + 1) * GN],
                                        pM[:, 0:FW].rearrange("p (k h n) -> p k h n", k=3, n=GN)).then_inc(zt_emptied, 1)

                                ch.step(dve.tensor_copy(nMo[:, :], nM[:, bass.ds(b, 1), :].rearrange("p a g -> p (a g)")))
                                neq(0)
                                for j in range(GB):
                                    if j + 1 < GB:
                                        neq(j + 1)
                                    dve.wait_ge(s_done, it * GB + j + 1)
                                    ch.step(dve.tensor_reduce(nmx[:, j:j + 1], pS[:, :, 0:SH], AX.XY, ALU.max, negate=True))
                                    dve.tensor_tensor(nMn[:, j:j + 1], nmx[:, j:j + 1], nMo[:, j:j + 1], ALU.min
                                                      ).then_inc(max_done, 1)
                                    for q, (t0, t1) in enumerate(pt_parts):
                                        dve.wait_ge(pt_filled, (it * GB + j) * 2 + q + 1)
                                        dve.tensor_copy(PT[:, t0:t1, :], pPT[q][:, 0:(t1 - t0) * P].rearrange(
                                            "p (t r) -> p t r", r=P)).then_inc(pt_emptied, 1)
                                    if j >= 1:
                                        zt_out(j - 1)
                                    if j == 0:
                                        dve.tensor_copy(qrow[:, :, :], qT[:, :, bass.ds((b + 1) * P, P)]).then_inc(qb_ready, 1)
                                dve.wait_ge(max_done, it * GB + GB)
                                dve.tensor_sub(dM[:, :], nMn[:, :], nMo[:, :]).then_inc(dM_done, 1)
                                ch.step(dve.tensor_copy(nM[:, bass.ds(b, 1), :].rearrange("p a g -> p (a g)"), nMn[:, :]))
                                dve.wait_ge(neq_done, it * GB + GB)
                                ch.step(dve.tensor_scalar(nid[:, :], nid[:, :], float(P), None, ALU.add))
                                dve.wait_ge(corr_done, it + 1)
                                dve.tensor_tensor(cdiag[:, :, :], corr[:, :, None].to_broadcast([P, GB, GN]),
                                                  seln[:, None, :].to_broadcast([P, GB, GN]), ALU.mult).then_inc(cdiag_done, 1)
                                zt_out(GB - 1)
                                dve.wait_ge(proj_done, it + 1)
                                Ub = U[:, bass.ds(b, 1), :].rearrange("p a (h c) -> p (a h) c", c=CW)
                                ch.step(dve.tensor_tensor(Utmp[:, :, :], Ub,
                                                          pM[:, H * CW:H * CW + H][:, :, None].to_broadcast([P, H, CW]), ALU.mult))
                                ch.step(dve.tensor_tensor(Ub, Utmp[:, :, :],
                                                          pM[:, 0:H * CW].rearrange("p (h c) -> p h c", c=CW), ALU.add))
                                dve.sem_inc(merged, 1)
                                assert ch.n == BATCH, ch.n
                            ch.base, ch.n = pbase + NB * BATCH + base, 0
                            ch.step(dve.tensor_scalar(nid[:, :], nid[:, :], float(-NP), None, ALU.add))
                            ch.step(dve.tensor_scalar(offs[:, :], offs[:, :], float(CH), float(E), ALU.add, ALU.min))
                            dve.sem_inc(pass_ready, 1)

                    @block.scalar
                    def _(act):
                        def empty_ring(n, value, dst, src):
                            act.wait_ge(ring_filled, value)
                            act.activation(dst, src, ACT.Copy).then_inc(ring_emptied, 1)

                        def g_piece(n, value):
                            k, r = G_PIECES[n]
                            rows = P if k < KD else DE + 1
                            empty_ring(n, value,
                                       G[0:rows, k, :, :].rearrange("p g (c r n) -> p r c g n", c=KD, r=HR)[:, r],
                                       ring[n % 2][0:rows, 0:KD * P].rearrange("p (c g n) -> p c g n", g=GB, n=GN))

                        act.wait_ge(consts2, CONSTS2)
                        for n in range(NG_P):
                            g_piece(n, n + 1)
                        with long_loop(act) as e0:
                            ps = e0 // CH
                            with act.Fori(0, NB) as b:
                                it = act.snap(ps * NB + b)
                                rb = act.snap(it * RING + NG_P)

                                def ft_out(j, t):
                                    n = j * T + t
                                    empty_ring(n, rb + (n + 1), FT[j % 2][:, :, t * P:(t + 1) * P],
                                               ring[n % 2][:, 0:FW].rearrange("p (k e) -> p k e", e=P))

                                def z_evac(j):
                                    act.wait_ge(slot_free, it * GB + (SLOTS + j + 1))
                                    act.activation(Zs[:, 0:ZW], pZ[:, 0:ZW], ACT.Copy).then_inc(z_out, 1)

                                for t in range(T):
                                    ft_out(0, t)
                                for j in range(GB):
                                    for t in range(T):
                                        if t == 2:
                                            act.wait_ge(max_done, it * GB + j + 1)
                                            act.activation(Pw[:, :].rearrange("p (a e) -> p a e", a=2), pS[:, :, 0:SH], ACT.Exp,
                                                           bias=nMn[:, j:j + 1]).then_inc(p_done, 1)
                                        if t == T - 1 and j >= 1:
                                            z_evac(j - 1)
                                        if j < GB - 1:
                                            ft_out(j + 1, t)
                                        else:
                                            for n in piece_share(t):
                                                g_piece(n, rb + (GB * T + n + 1))
                                act.wait_ge(dM_done, it + 1)
                                act.activation(corr[:, :], dM[:, :], ACT.Exp).then_inc(corr_done, 1)
                                z_evac(GB - 1)

                    @block.tensor
                    def _(pe):
                        def g_piece(n):
                            k, r = G_PIECES[n]
                            rows = P if k < KD else DE + 1
                            r0 = r * C
                            for c in range(KD):
                                w = Wk[r0:r0 + C, c, k * P:(k + 1) * P] if k < KD else W3[r0:r0 + C, c, :]
                                m = pe.matmul(ring[n % 2][0:rows, c * P:(c + 1) * P], w,
                                              qrow[r0:r0 + C, c, :], start=True, stop=True)
                            m.then_inc(ring_filled, 1)

                        pe.wait_ge(w2_landed, 16 * NW2)
                        pe.wait_ge(consts2, CONSTS2)
                        pe.wait_ge(qb_ready, 1)
                        for n in range(NG_P):
                            if n >= 2:
                                pe.wait_ge(ring_emptied, n - 1)
                            g_piece(n)

                        with long_loop(pe) as e0:
                            ps = e0 // CH
                            with pe.Fori(0, NB) as b:
                                it = pe.snap(ps * NB + b)
                                rb = pe.snap(it * RING + NG_P)

                                def ft(j, t):
                                    n = j * T + t
                                    if t == 0:
                                        s, u = j % SLOTS, j // SLOTS + 1
                                        pe.wait_ge(gathered[s], it * (16 * T * USES) + 16 * T * u)
                                        pe.wait_ge(ea_landed[s], it * (16 * USES) + 16 * u)
                                        pe.wait_ge(neq_done, it * GB + j + 1)
                                    pe.wait_ge(ring_emptied, rb + (n - 1))
                                    for k in range(3):
                                        m = pe.transpose(ring[n % 2][:, k * P:(k + 1) * P], F[j % SLOTS][:, t, k * P:(k + 1) * P],
                                                         ident[:, :])
                                    m.then_inc(ring_filled, 1)

                                def scores(j):
                                    pe.wait_ge(ring_emptied, rb + (j + 1) * T)
                                    pe.wait_ge(p_done, it * GB + j)
                                    for q in range(2):
                                        for k in range(3):
                                            rows = P if k < KD else K3
                                            m = pe.matmul(pS[:, q, 0:SH],
                                                          G[0:rows, k, j, :],
                                                          FT[j % 2][0:rows, k, q * SH:(q + 1) * SH],
                                                          start=(k == 0), stop=(k == 2))
                                    m.then_inc(s_done, 1)

                                def z_tile(j, t):
                                    if t == 0:
                                        pe.wait_ge(pt_emptied, (it * GB + j + 1) * 2)
                                        pe.wait_ge(z_out, it * GB + j)
                                    m = pe.matmul(pZ[:, 0:ZW], PT[:, t, :], F[j % SLOTS][:, t, 0:ZW],
                                                  start=(t == 0), stop=(t == T - 1))
                                    if t == T - 1:
                                        m.then_inc(slot_free, 1)

                                def pt(j):
                                    pe.wait_ge(p_done, it * GB + j + 1)
                                    for q, (t0, t1) in enumerate(pt_parts):
                                        pe.wait_ge(pt_emptied, (it * GB + j) * 2 + q)
                                        for t in range(t0, t1):
                                            m = pe.transpose(pPT[q][:, (t - t0) * P:(t - t0 + 1) * P],
                                                             Pw[:, t * P:(t + 1) * P], ident[:, :])
                                        m.then_inc(pt_filled, 1)

                                def zt(j):
                                    pe.wait_ge(z_out, it * GB + j + 1)
                                    pe.wait_ge(zt_emptied, it * GB + j)
                                    for k in range(3):
                                        m = pe.transpose(pM[:, k * P:(k + 1) * P], Zs[:, k * P:(k + 1) * P], ident[:, :])
                                    m.then_inc(zt_filled, 1)

                                for t in range(T):
                                    ft(0, t)
                                for j in range(GB):
                                    scores(j)
                                    if j == GB - 1:
                                        pe.wait_ge(qb_ready, it + 2)
                                    for t in range(T):
                                        if j >= 1:
                                            z_tile(j - 1, t)
                                        if j < GB - 1:
                                            ft(j + 1, t)
                                        else:
                                            for n in piece_share(t):
                                                pe.wait_ge(ring_emptied, rb + (GB * T + n - 1))
                                                g_piece(n)
                                    pt(j)
                                    if j == 1:
                                        pe.wait_ge(merged, it)
                                    if j >= 1:
                                        zt(j - 1)
                                for t in range(T):
                                    z_tile(GB - 1, t)
                                zt(GB - 1)
                                pe.wait_ge(zt_emptied, it * GB + GB)
                                for h in range(H):
                                    for k in range(3):
                                        rows = P if k < KD else DE + 1
                                        pe.matmul(pM[:, h * CW:(h + 1) * CW], ZT[0:rows, k, h, :], WvT[0:rows, k, h, :],
                                                  start=(k == 0), stop=(k == 2))
                                pe.wait_ge(cdiag_done, it + 1)
                                pe.matmul(pM[:, H * CW:H * CW + H], cdiag[:, :, :].rearrange("p g n -> p (g n)"), selh[:, :],
                                          start=True, stop=True).then_inc(proj_done, 1)


        with ExitStack() as s3:
            W = W7
            xnb = sbt(s3, "xnb", [P, W, D])
            xb = sbt(s3, "xb", [P, W, D])
            ob = sbt(s3, "ob", [P, W, D])
            db = sbt(s3, "db", [P, W, D])
            tb = sbt(s3, "tb", [P, W, D])
            yb = sbt(s3, "yb", [P, W, D])
            accb = sbt(s3, "accb", [P, W, D])
            rT = sbt(s3, "rT", [P, KD, W * P])
            h1 = sbt(s3, "h1", [P, KH, 4 * P])
            sh1 = sbt(s3, "sh1", [P, KD, 4 * P])
            sh2 = sbt(s3, "sh2", [P, 4 * P])
            e1 = sbt(s3, "e1", [P, NE, 4 * P])
            e2 = sbt(s3, "e2", [EH2 + 1, NE, 4 * P])
            WskT = sbt(s3, "WskT", [P, KD, D])
            W1T = sbt(s3, "W1T", [P, KD, HID])
            W2T = sbt(s3, "W2T", [P, KH, D])
            sW1 = sbt(s3, "sW1", [P, KD, D])
            sW2 = sbt(s3, "sW2", [P, KD, P])
            sW3 = sbt(s3, "sW3", [P, D])
            eW1 = sbt(s3, "eW1", [P, KD, NE, P])
            eW2 = sbt(s3, "eW2", [P, NE, EH2])
            eW3 = sbt(s3, "eW3", [EH2 + 1, NE, D])
            gW = sbt(s3, "gW", [P, KD, NE])
            rows = sbt(s3, "rows", [1, 3 * D + NE])
            b1c = sbt(s3, "b1c", [P, KH])
            sb1c = sbt(s3, "sb1c", [P, KD])
            sb2c = sbt(s3, "sb2c", [P, 1])
            eb1c = sbt(s3, "eb1c", [P, NE])
            eb2c = sbt(s3, "eb2c", [EH2, NE])
            lnp = sbt(s3, "lnp", [P, 4, D])
            wbt = sbt(s3, "wbt", [P, 3, D])
            w12 = sbt(s3, "w12", [P, D])
            w23 = sbt(s3, "w23", [P, D])
            eps3 = sbt(s3, "eps3", [P, 1])
            tri = sbt(s3, "tri", [P, NE, NE])
            rl = sbt(s3, "rl", [P, W * H])
            st3 = sbt(s3, "st3", [P, W, 6])
            mn3 = sbt(s3, "mn3", [P, W])
            vr3 = sbt(s3, "vr3", [P, W])
            lv3 = sbt(s3, "lv3", [P, W])
            rs3 = sbt(s3, "rs3", [P, W])
            zb = sbt(s3, "zb", [P, W])
            ezb = sbt(s3, "ezb", [P, W])
            g4 = sbt(s3, "g4", [P, W, NE])
            gx = sbt(s3, "gx", [P, W, NE])
            gs = sbt(s3, "gs", [P, W])
            c1 = sbt(s3, "c1", [P, W, NE, NE])
            c2 = sbt(s3, "c2", [P, W, NE, NE])
            rank = sbt(s3, "rank", [P, W, NE])
            we = sbt(s3, "we", [P, W, NE])
            tr = [pst(s3, f"tr{i}", [P, 4 * P]) for i in range(2)]
            hid = [pst(s3, f"hid{i}", [P, 4 * P]) for i in range(2)]
            nat = [pst(s3, f"nat{i}", [P, 4 * P]) for i in range(2)]
            pg = pst(s3, "pg", [P, 4 * P])

            parts = [(t0, min(t0 + 4, W)) for t0 in range(0, W, 4)]
            NPT = len(parts)
            HIDN = NPT * (KH + KD + 1 + 2 * NE)
            NATN = W * (3 + NE)
            w3_landed, consts3, rows_set = sem("w3_landed"), sem("consts3"), sem("rows_set")
            xn_landed, xb_landed, xn_used, x_used, out_ready, out_stored = (
                sem("xn_landed3"), sem("xb_landed3"), sem("xn_used3"), sem("x_used3"), sem("out_ready"), sem("out_stored"))
            tr_filled, tr_emptied = sem("tr_f3"), sem("tr_e3")
            hid_filled, hid_emptied = sem("hid_f3"), sem("hid_e3")
            nat_filled, nat_emptied = sem("nat_f3"), sem("nat_e3")
            z_ready, ez_ready, var_ready, rstd_ready = sem("z_ready"), sem("ez_ready"), sem("var_ready3"), sem("rstd_ready3")
            y_ready, m_ready, pg_filled, gl_ready, ge_ready = (
                sem("y_ready"), sem("m_ready"), sem("pg_filled"), sem("gl_ready"), sem("ge_ready"))
            out_v = out
            full, tail = N // P, N % P

            with nc.Block() as block:
                @block.sync
                def _(sp):
                    loads = [
                        (WskT[:, :, :], a["WskipT"].rearrange("(k p) c -> p k c", p=P)),
                        (rows[:, 0:D], a["bskip"].rearrange("(a n) -> a n", a=1)),
                        (rows[:, D:2 * D], a["b2"].rearrange("(a n) -> a n", a=1)),
                        (rows[:, 2 * D:3 * D], a["sb3"].rearrange("(a n) -> a n", a=1)),
                        (rows[:, 3 * D:3 * D + NE], a["gb"].rearrange("(a n) -> a n", a=1)),
                        (wbt[:, :, :], a["Wbeta"].rearrange("(k d) -> k d", k=3).partition_broadcast(P)),
                        (lnp[:, 0, :], a["ln1_g"].partition_broadcast(P)),
                        (lnp[:, 1, :], a["ln1_b"].partition_broadcast(P)),
                        (lnp[:, 2, :], a["ln2_g"].partition_broadcast(P)),
                        (lnp[:, 3, :], a["ln2_b"].partition_broadcast(P)),
                        (W1T[:, :, :], a["W1T"].rearrange("(k p) c -> p k c", p=P)),
                        (W2T[:, :, :], a["W2T"].rearrange("(k p) c -> p k c", p=P)),
                        (b1c[:, :], a["b1"]),
                        (sW1[:, :, :], a["sW1"].rearrange("(k p) c -> p k c", p=P)),
                        (sW2[:, :, :], a["sW2"].rearrange("(k p) c -> p k c", p=P)),
                        (sW3[:, :], a["sW3"]),
                        (sb1c[:, :], a["sb1"]),
                        (sb2c[:, :], a["sb2"].rearrange("(p o) -> p o", o=1)),
                        (eb1c[:, :], a["eb1"]),
                        (eb2c[:, :], a["eb2"]),
                        (eW3[EH2:EH2 + 1, :, :], a["eb3"].rearrange("(a e) d -> a e d", a=1)),
                        (eW2[:, :, :], a["eW2"].rearrange("e p c -> p e c")),
                        (eW3[0:EH2, :, :], a["eW3"].rearrange("e p c -> p e c")),
                        (gW[:, :, :], a["gW"].rearrange("(k p) e -> p k e", p=P)),
                    ] + [(eW1[:, k, :, :], a["eW1"][:, k * P:(k + 1) * P, :].rearrange("e p c -> p e c")) for k in range(KD)]
                    assert len(loads) == NW3
                    for dst, src in loads:
                        sp.dma_start(dst, src).then_inc(w3_landed, 16)
                    with sp.Fori(0, N7) as i:
                        sp.wait_ge(xn_used, i)
                        sp.dma_start(xnb[:, :, :], xn_v[:, bass.ds(i * W, W), :]).then_inc(xn_landed, 16)
                        sp.wait_ge(x_used, i)
                        sp.dma_start(xb[:, :, :], x_d[:, bass.ds(i * W, W), :]).then_inc(xb_landed, 16)

                @block.gpsimd
                def _(pool):
                    pool.memset(tri[:, :, :], 1.0).then_inc(consts3, 1)
                    pool.wait_ge(consts3, 1)
                    pool.affine_select(out=tri[:, :, :], in_=tri[:, :, :], compare_op=ALU.is_ge, fill=0.0, base=-1,
                                       pattern=[[1, NE], [-1, NE]], channel_multiplier=0).then_inc(consts3, 1)
                    if N7 > 1:
                        with pool.Fori(0, N7 - 1) as i:
                            pool.wait_ge(out_ready, i + 1)
                            pool.dma_start(out[bass.ds(i * W * P, W * P), :].rearrange("(j p) d -> p j d", p=P), accb[:, :, :]
                                           ).then_inc(out_stored, 16)
                    pool.wait_ge(out_ready, N7)
                    r0 = (N7 - 1) * W * P
                    whole = (N - r0) // P
                    last = N - r0 - whole * P
                    if whole:
                        pool.dma_start(out[r0:r0 + whole * P, :].rearrange("(j p) d -> p j d", p=P), accb[:, 0:whole, :]
                                       ).then_inc(out_stored, 16)
                    if last:
                        pool.dma_start(out[r0 + whole * P:N, :], accb[0:last, whole, :]).then_inc(out_stored, 16)
                    pool.wait_ge(out_stored, 16 * (N7 - 1 + (whole > 0) + (last > 0)))

                @block.vector
                def _(dve):
                    ch = Chain(dve, "dve3")
                    dve.memset(eps3[:, :], LN_EPS).then_inc(rows_set, 1)
                    dve.memset(e2[EH2:EH2 + 1, :, :], 1.0).then_inc(rows_set, 1)
                    dve.wait_ge(w3_landed, 16 * NW3)
                    dve.wait_ge(consts3, 2)
                    ch.step(dve.tensor_add(w12[:, :], wbt[:, 0, :], wbt[:, 1, :]))
                    ch.step(dve.tensor_sub(w23[:, :], wbt[:, 1, :], wbt[:, 2, :]))
                    base = ch.n
                    with dve.Fori(0, N7) as i:
                        ch.base, ch.n = dve.snap(i * DVE3 + base), 0
                        nat_i = dve.snap(i * NATN)
                        lns = [0]

                        def wide(v):
                            return v[:, None, :].to_broadcast([P, W, D])

                        def tiles(v):
                            return v[:, :, None].to_broadcast([P, W, D])

                        def layernorm(dst, src):
                            for j in range(W):
                                s = dve.bn_stats(st3[:, j, :], src[:, j, :])
                            ch.step(s)
                            mean_and_var(dve, ch, st3, mn3, vr3, D)
                            dve.sem_inc(var_ready, 1)
                            lns[0] += 1
                            dve.wait_ge(rstd_ready, i * 6 + 2 * lns[0])
                            for j in range(W):
                                s = dve.tensor_scalar(dst[:, j, :], src[:, j, :], mn3[:, j:j + 1], rs3[:, j:j + 1],
                                                      ALU.subtract, ALU.mult)
                            return s

                        Ub = U[:, bass.ds(i * W, W), :].rearrange("p a (h c) -> p (a h) c", c=CW)
                        ch.step(dve.tensor_scalar(rl[:, :], Ub[:, :, C], 1e-16, None, ALU.add))
                        ch.step(dve.reciprocal(rl[:, :], rl[:, :]))
                        ch.step(dve.tensor_tensor(ob[:, :, :].rearrange("p a (h c) -> p (a h) c", c=C), Ub[:, :, 0:C],
                                                  rl[:, :, None].to_broadcast([P, W * H, C]), ALU.mult))
                        for j in range(W):
                            dve.wait_ge(nat_filled, nat_i + (j + 1))
                            dve.tensor_sub(db[:, j, :], nat[j % 2][:, 0:D], ob[:, j, :]).then_inc(nat_emptied, 1)
                        dve.wait_ge(nat_emptied, nat_i + W)
                        ch.step(dve.tensor_tensor(tb[:, :, :], ob[:, :, :], wide(w12), ALU.mult))
                        ch.step(dve.tensor_tensor(yb[:, :, :], db[:, :, :], wide(w23), ALU.mult))
                        ch.step(dve.tensor_add(tb[:, :, :], tb[:, :, :], yb[:, :, :]))
                        dve.tensor_reduce(zb[:, :], tb[:, :, :], AX.X, ALU.add).then_inc(z_ready, 1)
                        dve.wait_ge(ez_ready, i + 1)
                        ch.step(dve.tensor_scalar(ezb[:, :], ezb[:, :], 1.0, None, ALU.add))
                        ch.step(dve.reciprocal(ezb[:, :], ezb[:, :]))
                        ch.step(dve.tensor_tensor(tb[:, :, :], db[:, :, :], tiles(ezb), ALU.mult))
                        ch.step(dve.tensor_add(tb[:, :, :], tb[:, :, :], ob[:, :, :]))
                        dve.wait_ge(xn_landed, i * 16 + 16)
                        ch.step(dve.tensor_add(tb[:, :, :], tb[:, :, :], xnb[:, :, :]))
                        dve.sem_inc(xn_used, 1)
                        ch.step(layernorm(db, tb))
                        ch.step(dve.tensor_tensor(db[:, :, :], db[:, :, :], wide(lnp[:, 0, :]), ALU.mult))
                        dve.tensor_tensor(yb[:, :, :], db[:, :, :], wide(lnp[:, 1, :]), ALU.add).then_inc(y_ready, 1)
                        dve.wait_ge(y_ready, i + 1)
                        for j in range(W):
                            n = W + j
                            dve.wait_ge(nat_filled, nat_i + (n + 1))
                            dve.tensor_add(tb[:, j, :], nat[n % 2][:, 0:D], yb[:, j, :]).then_inc(nat_emptied, 1)
                        dve.wait_ge(nat_emptied, nat_i + 2 * W)
                        ch.step(layernorm(db, tb))
                        ch.step(dve.tensor_tensor(db[:, :, :], db[:, :, :], wide(lnp[:, 2, :]), ALU.mult))
                        ch.step(dve.tensor_tensor(db[:, :, :], db[:, :, :], wide(lnp[:, 3, :]), ALU.add))
                        dve.wait_ge(xb_landed, i * 16 + 16)
                        ch.step(dve.tensor_add(tb[:, :, :], db[:, :, :], xb[:, :, :]))
                        dve.sem_inc(x_used, 1)
                        layernorm(yb, tb).then_inc(m_ready, 1)
                        dve.wait_ge(pg_filled, i + 1)
                        lg = pg[:, 0:W * NE].rearrange("p (w e) -> p w e", e=NE)
                        four = lambda v: v[:, :, None].to_broadcast([P, W, NE])
                        ch.step(dve.tensor_reduce(gs[:, :], lg, AX.X, ALU.max))
                        dve.tensor_tensor(g4[:, :, :], lg, four(gs), ALU.subtract).then_inc(gl_ready, 1)
                        dve.wait_ge(ge_ready, 2 * i + 1)
                        ch.step(dve.tensor_reduce(gs[:, :], gx[:, :, :], AX.X, ALU.add))
                        ch.step(dve.reciprocal(gs[:, :], gs[:, :]))
                        ch.step(dve.tensor_tensor(g4[:, :, :], gx[:, :, :], four(gs), ALU.mult))
                        gj = g4[:, :, None, :].to_broadcast([P, W, NE, NE])
                        ge = g4[:, :, :, None].to_broadcast([P, W, NE, NE])
                        tr4 = tri[:, None, :, :].to_broadcast([P, W, NE, NE])
                        ch.step(dve.tensor_tensor(c1[:, :, :, :], gj, ge, ALU.is_gt))
                        ch.step(dve.tensor_tensor(c2[:, :, :, :], gj, ge, ALU.is_equal))
                        ch.step(dve.tensor_tensor(c2[:, :, :, :], c2[:, :, :, :], tr4, ALU.mult))
                        ch.step(dve.tensor_tensor(c1[:, :, :, :], c1[:, :, :, :], c2[:, :, :, :], ALU.add))
                        ch.step(dve.tensor_reduce(rank[:, :, :], c1[:, :, :, :], AX.X, ALU.add))
                        ch.step(dve.tensor_scalar(rank[:, :, :], rank[:, :, :], 1.5, None, ALU.is_lt))
                        ch.step(dve.tensor_reduce(gs[:, :], g4[:, :, :], AX.X, ALU.max))
                        dve.tensor_tensor(g4[:, :, :], g4[:, :, :], four(gs), ALU.subtract).then_inc(gl_ready, 1)
                        dve.wait_ge(ge_ready, 2 * i + 2)
                        ch.step(dve.tensor_tensor(we[:, :, :], gx[:, :, :], rank[:, :, :], ALU.mult))
                        ch.step(dve.tensor_reduce(gs[:, :], we[:, :, :], AX.X, ALU.add))
                        ch.step(dve.reciprocal(gs[:, :], gs[:, :]))
                        ch.step(dve.tensor_tensor(we[:, :, :], we[:, :, :], four(gs), ALU.mult))
                        dve.wait_ge(out_stored, i * 16)
                        for j in range(W):
                            n = 2 * W + j * (1 + NE)
                            dve.wait_ge(nat_filled, nat_i + (n + 1))
                            dve.tensor_add(accb[:, j, :], nat[n % 2][:, 0:D], tb[:, j, :]).then_inc(nat_emptied, 1)
                            for e in range(NE):
                                n += 1
                                dve.wait_ge(nat_emptied, nat_i + n)
                                dve.wait_ge(nat_filled, nat_i + (n + 1))
                                s = dve.scalar_tensor_tensor(out=accb[:, j, :], in0=nat[n % 2][:, 0:D], scalar=we[:, j, e:e + 1],
                                                             in1=accb[:, j, :], op0=ALU.mult, op1=ALU.add)
                                s.then_inc(nat_emptied, 1)
                        dve.wait_ge(nat_emptied, nat_i + NATN)
                        dve.sem_inc(out_ready, 1)
                        assert ch.n == DVE3, ch.n

                @block.scalar
                def _(act):
                    act.wait_ge(w3_landed, 16 * NW3)
                    act.wait_ge(rows_set, 2)
                    with act.Fori(0, N7) as i:
                        hid_i = act.snap(i * HIDN)
                        hn = [0]

                        def transposed(r):
                            for j in range(W):
                                act.wait_ge(tr_filled, i * (3 * W) + (r * W + j + 1))
                                act.activation(rT[:, :, j * P:(j + 1) * P], tr[j % 2][:, 0:KD * P].rearrange(
                                    "p (k n) -> p k n", n=P), ACT.Copy).then_inc(tr_emptied, 1)

                        def rstd(n):
                            act.wait_ge(var_ready, i * 3 + n)
                            act.activation(lv3[:, :], vr3[:, :], ACT.Ln, bias=eps3[:, 0:1]).then_inc(rstd_ready, 1)
                            act.wait_ge(rstd_ready, i * 6 + (2 * n - 1))
                            act.activation(rs3[:, :], lv3[:, :], ACT.Exp, scale=-0.5).then_inc(rstd_ready, 1)

                        def hidden(dst, func, bias, w, rws=P):
                            n = hn[0]
                            hn[0] += 1
                            act.wait_ge(hid_filled, hid_i + (n + 1))
                            act.activation(dst, hid[n % 2][0:rws, 0:w], func, bias=bias).then_inc(hid_emptied, 1)

                        transposed(0)
                        act.wait_ge(z_ready, i + 1)
                        act.activation(ezb[:, :], zb[:, :], ACT.Exp, scale=-1.0).then_inc(ez_ready, 1)
                        rstd(1)
                        transposed(1)
                        for t0, t1 in parts:
                            for k in range(KH):
                                hidden(h1[:, k, 0:(t1 - t0) * P], ACT.Gelu, b1c[:, k:k + 1], (t1 - t0) * P)
                        rstd(2)
                        rstd(3)
                        transposed(2)
                        for q in range(2):
                            act.wait_ge(gl_ready, 2 * i + (q + 1))
                            act.activation(gx[:, :, :], g4[:, :, :], ACT.Exp).then_inc(ge_ready, 1)
                        for t0, t1 in parts:
                            w = (t1 - t0) * P
                            for c in range(KD):
                                hidden(sh1[:, c, 0:w], ACT.Relu, sb1c[:, c:c + 1], w)
                            for e in range(NE):
                                hidden(e1[:, e, 0:w], ACT.Relu, eb1c[:, e:e + 1], w)
                            hidden(sh2[:, 0:w], ACT.Relu, sb2c[:, 0:1], w)
                            for e in range(NE):
                                hidden(e2[0:EH2, e, 0:w], ACT.Relu, eb2c[:, e:e + 1], w, EH2)
                        assert hn[0] == HIDN

                @block.tensor
                def _(pe):
                    pe.wait_ge(w3_landed, 16 * NW3)
                    pe.wait_ge(rows_set, 2)
                    with pe.Fori(0, N7) as i:
                        hid_i = pe.snap(i * HIDN)
                        nat_i = pe.snap(i * NATN)
                        hn, nn = [0], [0]

                        def transpose_rows(r, src, ready, value):
                            pe.wait_ge(ready, value)
                            for j in range(W):
                                pe.wait_ge(tr_emptied, i * (3 * W) + (r * W + j - (1 if j else 0)))
                                for k in range(KD):
                                    m = pe.transpose(tr[j % 2][:, k * P:(k + 1) * P], src[:, j, k * P:(k + 1) * P], ident[:, :])
                                m.then_inc(tr_filled, 1)

                        def hidden(rws, w, terms):
                            n = hn[0]
                            hn[0] += 1
                            pe.wait_ge(hid_emptied, hid_i + max(n - 1, 0))
                            for q, (l, r) in enumerate(terms):
                                m = pe.matmul(hid[n % 2][0:rws, 0:w], l, r, start=(q == 0), stop=(q == len(terms) - 1))
                            m.then_inc(hid_filled, 1)

                        def node_major(terms):
                            n = nn[0]
                            nn[0] += 1
                            pe.wait_ge(nat_emptied, nat_i + max(n - 1, 0))
                            for q, (l, r) in enumerate(terms):
                                m = pe.matmul(nat[n % 2][:, 0:D], l, r, start=(q == 0), stop=(q == len(terms) - 1))
                            m.then_inc(nat_filled, 1)

                        transpose_rows(0, xnb, xn_landed, i * 16 + 16)
                        for j in range(W):
                            pe.wait_ge(tr_emptied, i * (3 * W) + (j + 1))
                            node_major([(rT[:, k, j * P:(j + 1) * P], WskT[:, k, :]) for k in range(KD)]
                                       + [(onesrow[:, :], rows[:, 0:D])])
                        transpose_rows(1, yb, y_ready, i + 1)
                        for t0, t1 in parts:
                            w = (t1 - t0) * P
                            pe.wait_ge(tr_emptied, i * (3 * W) + (W + t1))
                            for c in range(KH):
                                hidden(P, w, [(W1T[:, k, c * P:(c + 1) * P], rT[:, k, t0 * P:t1 * P]) for k in range(KD)])
                            pe.wait_ge(hid_emptied, hid_i + hn[0])
                            for j in range(t1 - t0):
                                node_major([(h1[:, k, j * P:(j + 1) * P], W2T[:, k, :]) for k in range(KH)]
                                           + [(onesrow[:, :], rows[:, D:2 * D])])
                        transpose_rows(2, yb, m_ready, i + 1)
                        pe.wait_ge(tr_emptied, i * (3 * W) + 3 * W)
                        for j in range(W):
                            for k in range(KD):
                                pe.matmul(pg[:, j * NE:(j + 1) * NE], rT[:, k, j * P:(j + 1) * P], gW[:, k, :], start=(k == 0), stop=False)
                            m = pe.matmul(pg[:, j * NE:(j + 1) * NE], onesrow[:, :], rows[:, 3 * D:3 * D + NE], start=False, stop=True)
                        m.then_inc(pg_filled, 1)
                        for t0, t1 in parts:
                            w = (t1 - t0) * P
                            for c in range(KD):
                                hidden(P, w, [(sW1[:, k, c * P:(c + 1) * P], rT[:, k, t0 * P:t1 * P]) for k in range(KD)])
                            for e in range(NE):
                                hidden(P, w, [(eW1[:, k, e, :], rT[:, k, t0 * P:t1 * P]) for k in range(KD)])
                            pe.wait_ge(hid_emptied, hid_i + (hn[0] - NE))
                            hidden(P, w, [(sW2[:, k, :], sh1[:, k, 0:w]) for k in range(KD)])
                            for e in range(NE):
                                pe.wait_ge(hid_emptied, hid_i + (hn[0] - 1 - e - (NE - 1 - e)))
                                hidden(EH2, w, [(eW2[:, e, :], e1[:, e, 0:w])])
                            pe.wait_ge(hid_emptied, hid_i + hn[0])
                            for j in range(t1 - t0):
                                cols = slice(j * P, (j + 1) * P)
                                node_major([(sh2[:, cols], sW3[:, :]), (onesrow[:, :], rows[:, 2 * D:3 * D])])
                                for e in range(NE):
                                    node_major([(e2[:, e, cols], eW3[:, e, :])])
                        assert (hn[0], nn[0]) == (HIDN, NATN)


NW3 = 26
DVE3 = 56


def kernel(**inputs):
    import concourse.bacc as _bacc
    from concourse.bass_utils import run_bass_kernel_spmd as _run

    g = {k: np.asarray(v) for k, v in inputs.items()}
    N, D = g["x"].shape
    E, DE = g["edge_attr_64"].shape
    NP = -(-N // P) * P
    tiles = -(-int(E * 16 * 1.1) // (N * P))
    CH = tiles * P
    EP = -(-(E + CH) // P) * P
    x = np.zeros((NP, D), np.float32)
    x[:N] = g["x"]
    src = np.zeros(EP, np.int32)
    src[:E] = g["src"]
    dst = np.full(EP, 1 << 20, np.int32)
    dst[:E] = g["dst"]
    ea = np.zeros((EP, DE), np.float32)
    ea[:E] = g["edge_attr_64"]

    def T(w):
        return np.ascontiguousarray(np.swapaxes(w, -1, -2))

    def cols(v):
        return np.ascontiguousarray(v.reshape(-1, P).T)

    arrays = {
        "x": x, "src": src, "dst": dst, "dst_first": dst[::P].copy(), "edge_attr": ea,
        "WqT": T(g["L0_gnn_Wq"]), "bq": cols(g["L0_gnn_bq"]), "Wk": g["L0_gnn_Wk"],
        "W3": np.concatenate([g["L0_gnn_We"], g["L0_gnn_bk"][:, None]], axis=1),
        "WvT": T(g["L0_gnn_Wv"]), "bv": g["L0_gnn_bv"], "WeT": T(g["L0_gnn_We"]),
        "ones": np.ones(8, np.float32), "WskipT": T(g["L0_gnn_Wskip"]), "bskip": g["L0_gnn_bskip"],
        "Wbeta": g["L0_gnn_Wbeta"].reshape(-1), "W1T": T(g["L0_gnn_W1"]), "W2T": T(g["L0_gnn_W2"]),
    }
    for n in ("ln1_g", "ln1_b", "ln2_g", "ln2_b", "b1", "b2"):
        arrays[n] = g[f"L0_gnn_{n}"]
    for n in ("sW1", "sb1", "sW2", "sb2", "sW3", "sb3", "eW1", "eb1", "eW2", "eb2", "eW3", "eb3", "gW", "gb"):
        arrays[n] = g[f"L0_ffn_{n}"]
    arrays["b1"], arrays["sb1"] = cols(arrays["b1"]), cols(arrays["sb1"])
    arrays["eb1"], arrays["eb2"] = T(arrays["eb1"]), T(arrays["eb2"])

    nc = _bacc.Bacc("TRN2", target_bir_lowering=False, num_devices=1)
    maps, aps = {}, {}
    for name, v in arrays.items():
        maps[f"in_{name}"] = np.ascontiguousarray(v)
        aps[name] = nc.dram_tensor(f"in_{name}", v.shape, mybir.dt.from_np(v.dtype), kind="ExternalInput").ap()
    aps["tiles"], aps["edges"] = tiles, E
    out = nc.dram_tensor("out_dram", (N, D), F32, kind="ExternalOutput").ap()
    with nc.allow_non_contiguous_dma(reason="a few short rows of weights"):
        build(nc, aps, out)
    r = _run(nc, [maps], core_ids=[0])
    return r.results[0]["out_dram"]
```

```python
from contextlib import ExitStack

import numpy as np
import concourse.bass as bass
from concourse import mybir

F32 = mybir.dt.float32
I32 = mybir.dt.int32
U32 = mybir.dt.uint32
ALU = mybir.AluOpType
ACT = mybir.ActivationFunctionType
AX = mybir.AxisListType

P = 128
BIG = 1.0e30
FLOOR = 1.0e29
LN_EPS = 1e-5


def mean_and_var(dve, ch, stats, mean, var, n):
    ch.step(dve.tensor_tensor(mean[:, :], stats[:, :, 1], stats[:, :, 4], ALU.subtract))
    ch.step(dve.tensor_tensor(var[:, :], mean[:, :], mean[:, :], ALU.mult))
    ch.step(dve.scalar_tensor_tensor(out=var[:, :], in0=var[:, :], scalar=n / 4.0, in1=stats[:, :, 2], op0=ALU.mult, op1=ALU.add))
    ch.step(dve.tensor_tensor(var[:, :], var[:, :], stats[:, :, 5], ALU.add))
    ch.step(dve.tensor_scalar(var[:, :], var[:, :], 1.0 / n, None, ALU.mult))
    ch.step(dve.tensor_tensor(mean[:, :], stats[:, :, 1], stats[:, :, 4], ALU.add))
    ch.step(dve.tensor_scalar(mean[:, :], mean[:, :], 0.5, None, ALU.mult))


def build(nc, a, out):
    N = out.shape[0]
    D = a["x"].shape[1]
    NP = a["x"].shape[0]
    NB = NP // P
    H = 8
    C = D // H
    DE = a["edge_attr"].shape[1]
    GN = P // H
    GB = P // GN
    NG = NB * GB
    T = a["tiles"]
    CH = T * P
    E = a["edges"]
    NCH = a["dst"].shape[0] // P
    KD = D // P
    FW = 3 * P
    ONE = D + DE
    FP = -(-(ONE + 1) // 4) * 4
    K3 = DE + 1 + GN
    ZW = D + DE + 1
    CW = C + 1
    SCALE = 1.0 / float(np.sqrt(C))
    SLOTS = 4
    W7 = 7 if NB % 7 == 0 else 1
    N7 = NB // W7
    HID = a["W1T"].shape[1]
    KH = HID // P
    NE = a["gW"].shape[1]
    EH2 = a["eW2"].shape[2]
    BC = -(-(NG + 1) // P)

    xn_d = nc.dram_tensor("xn_rows", [NP, D], F32, kind="Internal").ap()
    bound_d = nc.dram_tensor("bounds", [BC * P], I32, kind="Internal").ap()
    x_d = a["x"].rearrange("(b p) d -> p b d", p=P)
    xn_v = xn_d.rearrange("(b p) d -> p b d", p=P)
    dst_rows = a["dst"].rearrange("(r c) -> r c", c=P)

    top = ExitStack()

    def sem(name):
        return top.enter_context(nc.semaphore(name))

    class Chain:

        def __init__(self, eng, name):
            self.eng, self.sem, self.n, self.base = eng, sem(name), 0, 0

        def step(self, ins):
            self.n += 1
            ins.then_inc(self.sem, 1)
            self.eng.wait_ge(self.sem, self.base + self.n)

    with top:
        def sbt(stack, name, shape, dt=F32):
            return stack.enter_context(nc.sbuf_tensor(name, shape, dt))

        def pst(stack, name, shape, dt=F32):
            return stack.enter_context(nc.psum_tensor(name, shape, dt))

        ident = sbt(top, "ident", [P, P])
        U = sbt(top, "U", [P, NB, H * CW])
        passes = sbt(top, "passes", [1, 1], I32)
        offs = sbt(top, "offs", [1, NG + GB], I32)

        consts_ready = sem("consts_ready")

        mid = ExitStack()
        with mid:
            qT = sbt(mid, "qT", [P, KD, NP + P])
            with ExitStack() as s1:
                x_all = sbt(s1, "x_all", [P, NB, D])
                xs = sbt(s1, "xs", [P, W7, D])
                xT = sbt(s1, "xT", [P, KD, W7 * P])
                stats = sbt(s1, "stats", [P, NB, 6])
                mean = sbt(s1, "mean", [P, NB])
                var = sbt(s1, "var", [P, NB])
                lnv = sbt(s1, "lnv", [P, NB])
                rstd = sbt(s1, "rstd", [P, NB])
                epsc = sbt(s1, "epsc", [P, 1])
                WqT = sbt(s1, "WqT", [P, KD, D])
                bq = sbt(s1, "bq", [P, KD])
                bqs = sbt(s1, "bqs", [P, KD])
                firsts = sbt(s1, "firsts", [P, NCH], I32)
                hits = sbt(s1, "hits", [P, NCH])
                hits2 = sbt(s1, "hits2", [P, P])
                bval = sbt(s1, "bval", [P, BC])
                cnt = sbt(s1, "cnt", [P, BC])
                rowi = sbt(s1, "rowi", [P, BC], I32)
                drow = sbt(s1, "drow", [P, BC, P], I32)
                cnt2 = sbt(s1, "cnt2", [P, BC])
                starti = sbt(s1, "starti", [P, BC], I32)
                srow = sbt(s1, "srow", [1, BC * P], I32)
                srowf = sbt(s1, "srowf", [1, BC * P])
                lens = sbt(s1, "lens", [1, NG])
                mlen = sbt(s1, "mlen", [1, 1])
                tp = [pst(s1, f"tp{i}", [P, KD, P]) for i in range(2)]
                pq = [pst(s1, f"pq{i}", [P, 4 * P]) for i in range(2)]

                x_landed, w_landed, first_landed = sem("x_landed"), sem("w_landed"), sem("first_landed")
                rows_gathered, bounds_stored, bounds_landed = sem("rows_g"), sem("bounds_stored"), sem("bounds_landed")
                tiles_seen, xs_free = sem("tiles_seen"), sem("xs_free")
                U_cleared = sem("U_cleared")
                store_turns1 = sem("store_turns1")
                stats_done, rstd_done, xn_ready, xn_stored = sem("stats_done"), sem("rstd_done"), sem("xn_ready"), sem("xn_st")
                tp_filled, tp_emptied, q_filled, q_emptied = sem("tp_f"), sem("tp_e"), sem("q_f"), sem("q_e")
                bval_ready, rowi_ready, start_ready = sem("bval_r"), sem("rowi_r"), sem("start_r")
                q_steps = [(h0, min(4, W7 - h0)) for h0 in range(0, W7, 4)]
                Q7 = len(q_steps) * KD

                with nc.Block() as block:
                    @block.sync
                    def _(sp):
                        sp.dma_start(firsts[:, :], a["dst_first"].partition_broadcast(P)).then_inc(first_landed, 16)
                        sp.dma_start(x_all[:, :, :], x_d).then_inc(x_landed, 16)
                        sp.dma_start(WqT[:, :, :], a["WqT"].rearrange("(k p) c -> p k c", p=P)).then_inc(w_landed, 16)
                        sp.dma_start(bq[:, :], a["bq"]).then_inc(w_landed, 16)
                        sp.wait_ge(start_ready, 1)
                        sp.dma_start(bound_d.rearrange("(c p) -> p c", p=P), starti[:, :]).then_inc(bounds_stored, 16)
                        sp.wait_ge(bounds_stored, 16)
                        sp.dma_start(srow[:, :], bound_d.rearrange("(a n) -> a n", a=1)).then_inc(bounds_landed, 16)
                        sp.sem_inc(xs_free, 1)
                        with sp.Fori(0, N7) as i:
                            sp.wait_ge(xn_ready, (i + 1) * W7)
                            sp.sem_inc(store_turns1, 1)
                            sp.dma_start(xn_v[:, bass.ds(i * W7, W7), :], xs[:, :, :]).then_inc(xn_stored, 16)
                            sp.wait_ge(xn_stored, i * 16 + 16)
                            sp.sem_inc(xs_free, 1)
                        sp.wait_ge(xn_stored, 16 * N7)

                    @block.gpsimd
                    def _(pool):
                        pool.memset(ident[:, :], 0.0).then_inc(consts_ready, 1)
                        pool.iota(rowi[:, :], pattern=[[GN * P, BC]], base=0, channel_multiplier=GN).then_inc(bval_ready, 1)
                        pool.wait_ge(consts_ready, 1)
                        pool.affine_select(out=ident[:, :], in_=ident[:, :], compare_op=ALU.not_equal, fill=1.0,
                                           base=0, pattern=[[-1, P]], channel_multiplier=1).then_inc(consts_ready, 1)
                        pool.wait_ge(rowi_ready, 1)
                        for c in range(BC):
                            pool.indirect_dma_start(
                                out=drow[:, c, :], out_offset=None, in_=dst_rows,
                                in_offset=bass.IndirectOffsetOnAxis(ap=rowi[:, c:c + 1], axis=0),
                            ).then_inc(rows_gathered, 16)
                        pool.wait_ge(rows_gathered, 16 * BC)
                        pool.memset(U[:, :, :], 0.0).then_inc(U_cleared, 1)
                        pool.wait_ge(U_cleared, 1)

                    @block.vector
                    def _(dve):
                        ch = Chain(dve, "dve1")
                        ch.step(dve.memset(epsc[:, :], LN_EPS))
                        dve.wait_ge(bval_ready, 1)
                        ch.step(dve.tensor_copy(bval[:, :], rowi[:, :]))
                        dve.wait_ge(first_landed, 16)
                        for c in range(BC):
                            ch.step(dve.tensor_scalar(hits[:, :], firsts[:, :], bval[:, c:c + 1], 0.0, ALU.is_lt, ALU.add,
                                                      accum_out=cnt[:, c:c + 1]))
                        ch.step(dve.tensor_scalar(cnt[:, :], cnt[:, :], -1.0, 0.0, ALU.add, ALU.max))
                        ch.step(dve.tensor_copy(rowi[:, :], cnt[:, :]))
                        dve.sem_inc(rowi_ready, 1)
                        dve.wait_ge(rows_gathered, 16 * BC)
                        for c in range(BC):
                            ch.step(dve.tensor_scalar(hits2[:, :], drow[:, c, :], bval[:, c:c + 1], 0.0, ALU.is_lt, ALU.add,
                                                      accum_out=cnt2[:, c:c + 1]))
                        ch.step(dve.scalar_tensor_tensor(out=cnt[:, :], in0=cnt[:, :], scalar=float(P), in1=cnt2[:, :],
                                                         op0=ALU.mult, op1=ALU.add))
                        dve.tensor_copy(starti[:, :], cnt[:, :]).then_inc(start_ready, 1)
                        dve.wait_ge(bounds_landed, 16)
                        ch.step(dve.tensor_copy(srowf[:, :], srow[:, :]))
                        ch.step(dve.tensor_sub(lens[:, :], srowf[:, 1:NG + 1], srowf[:, 0:NG]))
                        ch.step(dve.tensor_reduce(mlen[:, :], lens[:, :], AX.X, ALU.max))
                        ch.step(dve.tensor_scalar(passes[:, :], mlen[:, :], 1.0, None, ALU.max))
                        ch.step(dve.tensor_scalar(offs[:, 0:NG], srowf[:, 0:NG], float(E), None, ALU.min))
                        dve.wait_ge(x_landed, 16)
                        with dve.Fori(0, N7) as i:
                            for j in range(W7):
                                m = i * W7 + j
                                dve.bn_stats(stats[:, bass.ds(m, 1), :].rearrange("p a d -> p (a d)"),
                                             x_all[:, bass.ds(m, 1), :].rearrange("p a d -> p (a d)")).then_inc(tiles_seen, 1)
                        dve.wait_ge(tiles_seen, NB)
                        mean_and_var(dve, ch, stats, mean, var, D)
                        dve.sem_inc(stats_done, 1)
                        dve.wait_ge(rstd_done, 2)
                        with dve.Fori(0, N7) as i:
                            dve.wait_ge(xs_free, i + 1)
                            dve.wait_ge(tp_filled, i * W7 + 1)
                            for j in range(W7):
                                m = i * W7 + j
                                dve.tensor_scalar(xs[:, j, :], x_all[:, bass.ds(m, 1), :].rearrange("p a d -> p (a d)"),
                                                  mean[:, bass.ds(m, 1)],
                                                  rstd[:, bass.ds(m, 1)], ALU.subtract, ALU.mult).then_inc(xn_ready, 1)

                    @block.scalar
                    def _(act):
                        ch = Chain(act, "act1")
                        act.sem_inc(q_emptied, 1)
                        act.wait_ge(stats_done, 1)
                        act.activation(lnv[:, :], var[:, :], ACT.Ln, bias=epsc[:, 0:1]).then_inc(rstd_done, 1)
                        act.wait_ge(rstd_done, 1)
                        act.activation(rstd[:, :], lnv[:, :], ACT.Exp, scale=-0.5).then_inc(rstd_done, 1)
                        act.wait_ge(w_landed, 32)
                        ch.step(act.mul(bqs[:, :], bq[:, :], SCALE))
                        with act.Fori(0, N7) as i:
                            for j in range(W7):
                                act.wait_ge(tp_filled, i * W7 + j + 2)
                                act.activation(xT[:, :, j * P:(j + 1) * P], tp[(j) % 2][:, :, :], ACT.Copy).then_inc(tp_emptied, 1)
                            for n, (h0, w) in enumerate(q_steps):
                                for c in range(KD):
                                    k = n * KD + c
                                    act.wait_ge(q_filled, i * Q7 + k + 1)
                                    act.activation(qT[:, c, bass.ds((i * W7 + h0) * P, w * P)], pq[k % 2][:, 0:w * P],
                                                   ACT.Identity, bias=bqs[:, c:c + 1], scale=SCALE).then_inc(q_emptied, 1)
                        act.wait_ge(q_emptied, N7 * Q7 + 1)
                        act.activation(qT[:, :, NP:NP + P], qT[:, :, 0:P], ACT.Copy)

                    @block.tensor
                    def _(pe):
                        pe.sem_inc(tp_filled, 1)
                        pe.wait_ge(consts_ready, 2)
                        pe.wait_ge(w_landed, 32)
                        with pe.Fori(0, N7) as i:
                            pe.wait_ge(q_emptied, i * Q7 + 1)
                            for j in range(W7):
                                pe.wait_ge(xn_ready, i * W7 + j + 1)
                                if j >= 2:
                                    pe.wait_ge(tp_emptied, i * W7 + j - 1)
                                for c in range(KD):
                                    t = pe.transpose(tp[j % 2][:, c, :], xs[:, j, c * P:(c + 1) * P], ident[:, :])
                                t.then_inc(tp_filled, 1)
                            for n, (h0, w) in enumerate(q_steps):
                                pe.wait_ge(tp_emptied, i * W7 + h0 + w)
                                for c in range(KD):
                                    k = n * KD + c
                                    if k >= 2:
                                        pe.wait_ge(q_emptied, i * Q7 + k)
                                    for f in range(KD):
                                        m = pe.matmul(pq[k % 2][:, 0:w * P], WqT[:, f, c * P:(c + 1) * P],
                                                      xT[:, f, h0 * P:(h0 + w) * P], start=(f == 0), stop=(f == KD - 1))
                                    m.then_inc(q_filled, 1)

            with ExitStack() as s2:
                F = [sbt(s2, f"F{i}", [P, T, FP]) for i in range(SLOTS)]
                F3 = [sbt(s2, f"F3{i}", [P, CH]) for i in range(SLOTS)]
                srci = [sbt(s2, f"srci{i}", [P, T], I32) for i in range(GB)]
                FT = [sbt(s2, f"FT{i}", [P, KD, CH]) for i in range(2)]
                G = sbt(s2, "G", [P, 3, GB, P])
                Pw = sbt(s2, "Pw", [P, T, P])
                PT = sbt(s2, "PT", [P, T, P])
                Zs = sbt(s2, "Zs", [P, FW])
                ZT = sbt(s2, "ZT", [P, 3, H, P])
                nM = sbt(s2, "nM", [P, NB, GB])
                nMo = sbt(s2, "nMo", [P, GB])
                nMn = sbt(s2, "nMn", [P, GB])
                nmx = sbt(s2, "nmx", [P, GB])
                dM = sbt(s2, "dM", [P, GB])
                corr = sbt(s2, "corr", [P, GB])
                cdiag = sbt(s2, "cdiag", [P, GB, GN])
                seln = sbt(s2, "seln", [P, GN])
                selh = sbt(s2, "selh", [P, H])
                nid = sbt(s2, "nid", [P, NG + 2])
                Wk = sbt(s2, "Wk", [P, KD, D])
                W3 = sbt(s2, "W3", [P, KD, DE + 1])
                WvT = sbt(s2, "WvT", [P, 3, H, CW])
                Utmp = sbt(s2, "Utmp", [P, H, CW])
                qh = [sbt(s2, f"qh{i}", [P, KD, P // C, P // 2]) for i in range(2)]
                hmask = sbt(s2, "hmask", [P, P // C])

                ring = [pst(s2, f"ring{i}", [P, 4 * P]) for i in range(2)]
                pS = pst(s2, "pS", [P, 2, 4 * P])
                pPT = [pst(s2, f"pPT{i}", [P, 4 * P]) for i in range(2)]
                pZ = pst(s2, "pZ", [P, 4 * P])
                pM = pst(s2, "pM", [P, 4 * P])

                SH = CH // 2
                TA = (T + 1) // 2
                pt_parts = [(0, TA), (TA, T)]
                HR = P // C
                G_PIECES = [(k, c) for k in range(3) for c in range(KD)]
                NPC = len(G_PIECES)
                HB = GB // 2

                def pieces(j):
                    half, first = (0, j - (HB - 1)) if HB - 1 <= j < GB - 1 else (1, (j + 1) % GB)
                    return [(half, i) for i in range(first * NPC // HB, (first + 1) * NPC // HB)]

                def ring_items(j):
                    items = [("ft", t) for t in range(T)]
                    for n, piece in enumerate(pieces(j)):
                        items.insert(2 * n + 1, piece)
                    early = len(items) - 2
                    cut = [-(-early * t // (T - 1)) for t in range(T)] + [len(items)]
                    return [items[cut[t]:cut[t + 1]] for t in range(T)]

                FIRST = [(0, i) for i in range(NPC)] + pieces(GB - 1)
                RBASE = [sum(T + len(pieces(i)) for i in range(j)) for j in range(GB + 1)]
                RB = RBASE[GB]
                RING0 = len(FIRST) + 2 * T
                assert RB % 2 == 0 and CH % 2 == 0 and SH <= 512 and GB == 2 * SLOTS

                w2_landed, wv_landed, consts2 = sem("w2_landed"), sem("wv_landed"), sem("consts2")
                idx_landed = [sem(f"idx_landed{i}") for i in range(GB)]
                f3_landed = [sem(f"f3_landed{i}") for i in range(SLOTS)]
                ea_landed = [sem(f"ea_landed{i}") for i in range(SLOTS)]
                gathered = [sem(f"gathered{i}") for i in range(SLOTS)]
                slot_free = sem("slot_free")
                load_turns, gather_turns = sem("load_turns"), sem("gather_turns")
                neq_done, pass_ready, qh_ready = sem("neq_done"), sem("pass_ready"), sem("qh_ready")
                ring_filled, ring_emptied = sem("ring_filled"), sem("ring_emptied")
                s_done, max_done, p_done = sem("s_done"), sem("max_done"), sem("p_done")
                pt_filled, pt_emptied = sem("pt_filled"), sem("pt_emptied")
                z_out, zt_filled, zt_emptied = sem("z_out"), sem("zt_filled"), sem("zt_emptied")
                dM_done, corr_done, cdiag_done, proj_done, merged = (
                    sem("dM_done"), sem("corr_done"), sem("cdiag_done"), sem("proj_done"), sem("merged"))

                NW2, NWV = 2, KD + 3
                CONSTS2 = 15 + H

                def long_loop(eng):
                    longest = eng.value_load(passes[0:1, 0:1], min_val=1, max_val=E)
                    return eng.Fori(0, longest, CH)

                with nc.Block() as block:
                    @block.sync
                    def _(sp):
                        def load_indices(o, j):
                            sp.dma_start(srci[j % GB][:, :], a["src"][bass.ds(o, CH)].rearrange("(p t) -> p t", t=T)
                                         ).then_inc(idx_landed[j % GB], 16)

                        def load_edges(o, j):
                            s = j % SLOTS
                            sp.dma_start(F3[s][DE:K3, :].bitcast(I32), a["dst"][bass.ds(o, CH)].partition_broadcast(K3 - DE)
                                         ).then_inc(f3_landed[s], 16)
                            sp.dma_start(F3[s][0:DE, :], a["edge_attrT"][:, bass.ds(o, CH)]).then_inc(f3_landed[s], 16)
                            sp.dma_start(F[s][:, :, D:D + DE],
                                         a["edge_attr"][bass.ds(o, CH), :].rearrange("(p t) d -> p t d", t=T)
                                         ).then_inc(ea_landed[s], 16)

                        def starts(first, n):
                            _, at = nc.values_load_multi_w_load_instructions(
                                offs[0:1, bass.ds(first, n)], engines=[mybir.EngineType.SP], min_val=0, max_val=E,
                                skip_runtime_bounds_check_because="clamped to E by the vector engine")
                            return at

                        sp.dma_start(Wk[:, :, :], a["Wk"].rearrange("(k p) f -> p k f", p=P)).then_inc(w2_landed, 16)
                        sp.dma_start(W3[:, :, :], a["W3"].rearrange("(k p) f -> p k f", p=P)).then_inc(w2_landed, 16)
                        sp.wait_ge(slot_free, SLOTS)
                        at = starts(0, 3)
                        for j in range(2):
                            load_indices(at[j], j)
                            load_edges(at[j], j)
                        load_indices(at[2], 2)
                        sp.wait_ge(consts2, 2)
                        for k in range(KD):
                            sp.dma_start(WvT[:, k, :, 0:C], a["WvT"][k * P:(k + 1) * P, :].rearrange("p (h c) -> p h c", h=H)
                                         ).then_inc(wv_landed, 16)
                        sp.dma_start(WvT[0:DE, KD, :, 0:C], a["WeT"].rearrange("p (h c) -> p h c", h=H)).then_inc(wv_landed, 16)
                        sp.dma_start(WvT[DE:DE + 1, KD, :, 0:C], a["bv"].rearrange("(a h c) -> a h c", a=1, h=H)
                                     ).then_inc(wv_landed, 16)
                        sp.dma_start(WvT[DE:DE + 1, KD, :, C:CW], a["ones"].rearrange("(a h c) -> a h c", a=1, h=H)
                                     ).then_inc(wv_landed, 16)
                        with long_loop(sp) as e0:
                            ps = e0 // CH
                            sp.wait_ge(pass_ready, ps + 1)
                            sp.sem_inc(load_turns, 1)
                            with sp.Fori(0, NB) as b:
                                it = sp.snap(ps * NB + b)
                                at = starts(b * GB + 2, GB + 1)
                                for j in range(GB):
                                    sp.wait_ge(slot_free, it * GB + (j + 3))
                                    sp.sem_inc(load_turns, 1)
                                    load_edges(at[j], j + 2)
                                    load_indices(at[j + 1], j + 3)
                            sp.wait_ge(idx_landed[2], (ps * NB + (NB + 1)) * 16)
                            sp.sem_inc(load_turns, 1)

                    @block.gpsimd
                    def _(pool):
                        pool.iota(nid[:, :], pattern=[[GN, NG + 2]], base=-(DE + 1), channel_multiplier=1,
                                  allow_small_or_imprecise_dtypes=True).then_inc(consts2, 1)
                        pool.memset(WvT[:, :, :, :], 0.0).then_inc(consts2, 1)
                        pool.memset(G[:, KD, :, :], 0.0).then_inc(consts2, 1)
                        pool.memset(seln[:, :], 0.0).then_inc(consts2, 1)
                        pool.memset(selh[:, :], 1.0).then_inc(consts2, 1)
                        pool.wait_ge(consts2, 5)
                        pool.iota(nid[:, NG:NG + 2], pattern=[[GN, 2]], base=-(DE + 1), channel_multiplier=1,
                                  allow_small_or_imprecise_dtypes=True).then_inc(consts2, 1)
                        pool.wait_ge(consts2, 6)
                        pool.memset(nid[DE:DE + 1, :], -1.0e6).then_inc(consts2, 1)
                        pool.wait_ge(consts2, 7)
                        g3 = G[:, KD, :, :].rearrange("p g (h n) -> p (g h) n", n=GN)
                        pool.affine_select(out=g3, in_=g3, compare_op=ALU.not_equal, fill=-BIG, base=-(DE + 1),
                                           pattern=[[0, H * GB], [-1, GN]], channel_multiplier=1).then_inc(consts2, 1)
                        for h in range(H):
                            pool.affine_select(out=seln[:, :], in_=seln[:, :], compare_op=ALU.not_equal, fill=1.0,
                                               base=-GN * h, pattern=[[-1, GN]], channel_multiplier=1).then_inc(consts2, 1)
                            pool.wait_ge(consts2, 9 + h)
                        pool.affine_select(out=selh[:, :], in_=selh[:, :], compare_op=ALU.is_ge, fill=0.0,
                                           base=0, pattern=[[-GN, H]], channel_multiplier=1).then_inc(consts2, 1)
                        pool.wait_ge(consts2, 9 + H)
                        pool.affine_select(out=selh[:, :], in_=selh[:, :], compare_op=ALU.is_ge, fill=0.0,
                                           base=GN - 1, pattern=[[GN, H]], channel_multiplier=-1).then_inc(consts2, 1)
                        pool.memset(hmask[:, :], 1.0).then_inc(consts2, 1)
                        pool.wait_ge(consts2, 11 + H)
                        pool.affine_select(out=hmask[:, :], in_=hmask[:, :], compare_op=ALU.is_ge, fill=0.0,
                                           base=0, pattern=[[-C, HR]], channel_multiplier=1).then_inc(consts2, 1)
                        pool.wait_ge(consts2, 12 + H)
                        pool.affine_select(out=hmask[:, :], in_=hmask[:, :], compare_op=ALU.is_ge, fill=0.0,
                                           base=C - 1, pattern=[[C, HR]], channel_multiplier=-1).then_inc(consts2, 1)
                        pool.wait_ge(consts2, 13 + H)
                        pool.sem_inc(consts2, 2)

                        def gather(j):
                            s = j % SLOTS
                            for t in range(T):
                                pool.indirect_dma_start(
                                    out=F[s][:, t, 0:D], out_offset=None, in_=xn_d,
                                    in_offset=bass.IndirectOffsetOnAxis(ap=srci[j % GB][:, t:t + 1], axis=0),
                                ).then_inc(gathered[s], 16)

                        for j in range(2):
                            pool.wait_ge(idx_landed[j], 16)
                            gather(j)
                        with long_loop(pool) as e0:
                            ps = e0 // CH
                            with pool.Fori(0, NB) as b:
                                it = pool.snap(ps * NB + b)
                                for j in range(GB):
                                    pool.wait_ge(slot_free, it * GB + (j + 3))
                                    pool.sem_inc(gather_turns, 1)
                                    first = 1 if j + 2 < GB else 2
                                    pool.wait_ge(idx_landed[(j + 2) % GB], it * 16 + 16 * first)
                                    pool.sem_inc(gather_turns, 1)
                                    gather(j + 2)

                    @block.vector
                    def _(dve):
                        ch = Chain(dve, "dve2")
                        for s in range(SLOTS):
                            dve.memset(F[s][:, :, ONE:ONE + 1], 1.0).then_inc(slot_free, 1)
                        ch.step(dve.memset(Zs[:, :], 0.0))
                        ch.step(dve.memset(nM[:, :, :], FLOOR))
                        dve.sem_inc(zt_emptied, 1)
                        dve.sem_inc(merged, 1)
                        ch.step(dve.tensor_scalar(offs[:, NG:NG + GB], offs[:, 0:GB], float(CH), float(E), ALU.add, ALU.min))
                        dve.sem_inc(pass_ready, 1)
                        dve.wait_ge(consts2, CONSTS2)

                        def neq(j, c, value):
                            dve.wait_ge(f3_landed[j], value)
                            dve.tensor_scalar(F3[j][DE:K3, :], F3[j][DE:K3, :].bitcast(I32), nid[DE:K3, c], None,
                                              ALU.not_equal).then_inc(neq_done, 1)

                        def maximum(j, value):
                            dve.wait_ge(s_done, value)
                            ch.step(dve.tensor_reduce(nmx[:, j:j + 1], pS[:, :, 0:SH], AX.XY, ALU.max, negate=True))
                            dve.tensor_tensor(nMn[:, j:j + 1], nmx[:, j:j + 1], nMo[:, j:j + 1], ALU.min).then_inc(max_done, 1)

                        def pt_out(value):
                            for q, (t0, t1) in enumerate(pt_parts):
                                dve.wait_ge(pt_filled, value + (q + 1))
                                dve.tensor_copy(PT[:, t0:t1, :], pPT[q][:, 0:(t1 - t0) * P].rearrange(
                                    "p (t r) -> p t r", r=P)).then_inc(pt_emptied, 1)

                        def spread(half, first):
                            for c in range(KD):
                                dve.tensor_tensor(qh[half][:, c, :, :],
                                                  qT[:, c, bass.ds(first, P // 2)][:, None, :].to_broadcast([P, HR, P // 2]),
                                                  hmask[:, :, None].to_broadcast([P, HR, P // 2]), ALU.mult).then_inc(qh_ready, 1)

                        for i in range(2):
                            spread(i, i * P // 2)
                        ch.step(dve.tensor_copy(nMo[:, :], nM[:, 0, :]))
                        for j in range(2):
                            neq(j, slice(j, j + 1), 32)
                        maximum(0, 1)
                        pt_out(0)
                        base = ch.n
                        BATCH = GB + 4
                        with long_loop(dve) as e0:
                            ps = e0 // CH
                            pbase = ps * (NB * BATCH + 2)
                            with dve.Fori(0, NB) as b:
                                it = dve.snap(ps * NB + b)
                                nb = dve.snap((b + 1) % NB)
                                ch.base, ch.n = dve.snap(pbase + b * BATCH + base), 0
                                for j in range(GB):
                                    neq((j + 2) % SLOTS, bass.ds(b * GB + (j + 2), 1), it * (32 * GB // SLOTS) + 32 * ((j + 2) // SLOTS + 1))
                                    if j == GB - 1:
                                        dve.wait_ge(max_done, it * GB + GB)
                                        dve.tensor_sub(dM[:, :], nMn[:, :], nMo[:, :]).then_inc(dM_done, 1)
                                        ch.step(dve.tensor_copy(nM[:, bass.ds(b, 1), :].rearrange("p a g -> p (a g)"), nMn[:, :]))
                                        dve.wait_ge(dM_done, it + 1)
                                        ch.step(dve.tensor_copy(nMo[:, :], nM[:, bass.ds(nb, 1), :].rearrange("p a g -> p (a g)")))
                                    maximum((j + 1) % GB, it * GB + (j + 2))
                                    if j == 0 or j == HB - 1:
                                        i = 0 if j == 0 else 1
                                        spread(i, (b + 1) * P + i * P // 2)
                                    def zt_out(j):
                                        dve.wait_ge(zt_filled, it * GB + (j + 1))
                                        dve.tensor_copy(
                                            ZT[:, :, :, j * GN:(j + 1) * GN],
                                            pM[:, 0:FW].rearrange("p (k h n) -> p k h n", k=3, n=GN)).then_inc(zt_emptied, 1)

                                    if j == GB - 1:
                                        zt_out(j)
                                    pt_out(it * (2 * GB) + 2 * (j + 1))
                                    if j < GB - 1:
                                        zt_out(j)
                                dve.wait_ge(corr_done, it + 1)
                                dve.tensor_tensor(cdiag[:, :, :], corr[:, :, None].to_broadcast([P, GB, GN]),
                                                  seln[:, None, :].to_broadcast([P, GB, GN]), ALU.mult).then_inc(cdiag_done, 1)
                                dve.wait_ge(proj_done, it + 1)
                                Ub = U[:, bass.ds(b, 1), :].rearrange("p a (h c) -> p (a h) c", c=CW)
                                ch.step(dve.tensor_tensor(Utmp[:, :, :], Ub,
                                                          pM[:, H * CW:H * CW + H][:, :, None].to_broadcast([P, H, CW]), ALU.mult))
                                ch.step(dve.tensor_tensor(Ub, Utmp[:, :, :],
                                                          pM[:, 0:H * CW].rearrange("p (h c) -> p h c", c=CW), ALU.add))
                                dve.sem_inc(merged, 1)
                                assert ch.n == BATCH, ch.n
                            ch.base, ch.n = pbase + NB * BATCH + base, 0
                            ch.step(dve.tensor_scalar(offs[:, 0:NG], offs[:, 0:NG], float(CH), float(E), ALU.add, ALU.min))
                            ch.step(dve.tensor_scalar(offs[:, NG:NG + GB], offs[:, 0:GB], float(CH), float(E), ALU.add, ALU.min))
                            dve.sem_inc(pass_ready, 1)

                    @block.scalar
                    def _(act):
                        def empty_ring(n, value, dst, src):
                            act.wait_ge(ring_filled, value)
                            act.activation(dst, src, ACT.Copy).then_inc(ring_emptied, 1)

                        def g_piece(half, i, n, value):
                            k, c = G_PIECES[i]
                            rows = P if k < KD else DE + 1
                            empty_ring(n, value,
                                       G[0:rows, k, half * HB:(half + 1) * HB, :].rearrange("p g (c r n) -> p c r g n", c=KD, r=HR)[:, c],
                                       ring[n % 2][0:rows, 0:HR * P // 2].rearrange("p (r g n) -> p r g n", g=HB, n=GN))

                        def ft_out(j, t, n, value):
                            empty_ring(n, value, FT[j % 2][:, :, :].rearrange("p k (e t) -> p t k e", t=T)[:, t],
                                       ring[n % 2][:, 0:D].rearrange("p (k e) -> p k e", e=P))

                        def weights(j, value):
                            act.wait_ge(max_done, value)
                            act.activation(Pw[:, :, :].rearrange("p t (a e) -> p a e t", a=2),
                                           pS[:, :, 0:SH].rearrange("p a (e t) -> p a e t", t=T), ACT.Exp,
                                           bias=nMn[:, j:j + 1]).then_inc(p_done, 1)

                        act.sem_inc(z_out, 1)
                        act.wait_ge(consts2, CONSTS2)
                        n = 0
                        for half, i in FIRST:
                            g_piece(half, i, n, n + 1)
                            n += 1
                        for j in range(2):
                            for t in range(T):
                                ft_out(j, t, n, n + 1)
                                n += 1
                        weights(0, 1)
                        with long_loop(act) as e0:
                            ps = e0 // CH
                            with act.Fori(0, NB) as b:
                                it = act.snap(ps * NB + b)
                                rb = act.snap(it * RB + RING0)
                                for j in range(GB):
                                    m = RBASE[j]
                                    for t, items in enumerate(ring_items(j)):
                                        if t == 1:
                                            weights((j + 1) % GB, it * GB + (j + 2))
                                        if t == T - 1:
                                            act.wait_ge(slot_free, it * GB + (SLOTS + j + 1))
                                            act.activation(Zs[:, 0:ZW], pZ[:, 0:ZW], ACT.Copy).then_inc(z_out, 1)
                                        for kind, i in items:
                                            if kind == "ft":
                                                ft_out(j, i, RING0 + m, rb + (m + 1))
                                            else:
                                                g_piece(kind, i, RING0 + m, rb + (m + 1))
                                            m += 1
                                    if j == GB - 1:
                                        act.wait_ge(dM_done, it + 1)
                                        act.activation(corr[:, :], dM[:, :], ACT.Exp).then_inc(corr_done, 1)
                                    assert m == RBASE[j + 1]

                    @block.tensor
                    def _(pe):
                        def g_piece(half, i, n):
                            k, c = G_PIECES[i]
                            rows = P if k < KD else DE + 1
                            w = Wk[:, c, k * P:(k + 1) * P] if k < KD else W3[:, c, :]
                            pe.matmul(ring[n % 2][0:rows, 0:HR * P // 2], w, qh[half][:, c, :, :].rearrange("p r n -> p (r n)"),
                                      start=True, stop=True).then_inc(ring_filled, 1)

                        def ft(j, t, n):
                            for k in range(KD):
                                m = pe.transpose(ring[n % 2][:, k * P:(k + 1) * P], F[j][:, t, k * P:(k + 1) * P], ident[:, :])
                            m.then_inc(ring_filled, 1)

                        def scores(j, s):
                            for q in range(2):
                                for k in range(3):
                                    f = FT[j % 2][:, k, q * SH:(q + 1) * SH] if k < KD else F3[s][0:K3, q * SH:(q + 1) * SH]
                                    m = pe.matmul(pS[:, q, 0:SH], G[0:(P if k < KD else K3), k, j, :], f,
                                                  start=(k == 0), stop=(k == 2))
                            m.then_inc(s_done, 1)

                        def pt():
                            for q, (t0, t1) in enumerate(pt_parts):
                                for t in range(t0, t1):
                                    m = pe.transpose(pPT[q][:, (t - t0) * P:(t - t0 + 1) * P], Pw[:, t, :], ident[:, :])
                                m.then_inc(pt_filled, 1)

                        pe.wait_ge(w2_landed, 16 * NW2)
                        pe.wait_ge(consts2, CONSTS2)
                        pe.wait_ge(qh_ready, 2 * KD)
                        n = 0
                        for half, i in FIRST:
                            if n >= 2:
                                pe.wait_ge(ring_emptied, n - 1)
                            g_piece(half, i, n)
                            n += 1
                        for j in range(2):
                            pe.wait_ge(gathered[j], 16 * T)
                            for t in range(T):
                                pe.wait_ge(ring_emptied, n - 1)
                                ft(j, t, n)
                                n += 1
                        pe.wait_ge(ring_emptied, n)
                        pe.wait_ge(neq_done, 1)
                        scores(0, 0)
                        pe.wait_ge(p_done, 1)
                        pt()
                        pe.wait_ge(wv_landed, 16 * NWV)

                        with long_loop(pe) as e0:
                            ps = e0 // CH
                            with pe.Fori(0, NB) as b:
                                it = pe.snap(ps * NB + b)
                                rb = pe.snap(it * RB + RING0)

                                def zt(j):
                                    if j == 0:
                                        pe.wait_ge(merged, it + 1)
                                    pe.wait_ge(zt_emptied, it * GB + (j + 1))
                                    pe.wait_ge(z_out, it * GB + (j + 2))
                                    for k in range(3):
                                        z = pe.transpose(pM[:, k * P:(k + 1) * P], Zs[:, k * P:(k + 1) * P], ident[:, :])
                                    z.then_inc(zt_filled, 1)

                                for j in range(GB):
                                    m = RBASE[j]
                                    s, s2 = j % SLOTS, (j + 2) % SLOTS
                                    pe.wait_ge(ring_emptied, rb + m)
                                    pe.wait_ge(neq_done, it * GB + (j + 2))
                                    pe.wait_ge(p_done, it * GB + (j + 1))
                                    scores((j + 1) % GB, (j + 1) % SLOTS)
                                    pe.wait_ge(pt_emptied, (it * GB + (j + 1)) * 2)
                                    pe.wait_ge(ea_landed[s], it * (16 * GB // SLOTS) + 16 * (j // SLOTS + 1))
                                    pe.wait_ge(z_out, it * GB + (j + 1))
                                    if j == HB - 1 or j == GB - 1:
                                        pe.wait_ge(qh_ready, it * (2 * KD) + (3 if j == HB - 1 else 4) * KD)
                                    for t, items in enumerate(ring_items(j)):
                                        z = pe.matmul(pZ[:, 0:ZW], PT[:, t, :], F[s][:, t, 0:ZW], start=(t == 0), stop=(t == T - 1))
                                        if t == T - 1:
                                            z.then_inc(slot_free, 1)
                                        if t == 0:
                                            pe.wait_ge(gathered[s2], it * (16 * T * GB // SLOTS) + 16 * T * ((j + 2) // SLOTS + 1))
                                        for kind, i in items:
                                            pe.wait_ge(ring_emptied, rb + (m - 1))
                                            if kind == "ft":
                                                ft(s2, i, RING0 + m)
                                            else:
                                                g_piece(kind, i, RING0 + m)
                                            m += 1
                                    if j == GB - 1:
                                        zt(j)
                                    pe.wait_ge(p_done, it * GB + (j + 2))
                                    pt()
                                    if j < GB - 1:
                                        zt(j)
                                pe.wait_ge(zt_emptied, it * GB + (GB + 1))
                                for h in range(H):
                                    for k in range(3):
                                        rows = P if k < KD else DE + 1
                                        pe.matmul(pM[:, h * CW:(h + 1) * CW], ZT[0:rows, k, h, :], WvT[0:rows, k, h, :],
                                                  start=(k == 0), stop=(k == 2))
                                pe.wait_ge(cdiag_done, it + 1)
                                pe.matmul(pM[:, H * CW:H * CW + H], cdiag[:, :, :].rearrange("p g n -> p (g n)"), selh[:, :],
                                          start=True, stop=True).then_inc(proj_done, 1)


        with ExitStack() as s3:
            W = W7
            xnb = sbt(s3, "xnb", [P, W, D])
            xb = sbt(s3, "xb", [P, W, D])
            ob = sbt(s3, "ob", [P, W, D])
            db = sbt(s3, "db", [P, W, D])
            tb = sbt(s3, "tb", [P, W, D])
            yb = sbt(s3, "yb", [P, W, D])
            accb = sbt(s3, "accb", [P, W, D])
            rT = sbt(s3, "rT", [P, KD, W * P])
            h1 = sbt(s3, "h1", [P, KH, 4 * P])
            sh1 = sbt(s3, "sh1", [P, KD, 4 * P])
            sh2 = sbt(s3, "sh2", [P, 4 * P])
            e1 = sbt(s3, "e1", [P, NE, 4 * P])
            e2 = sbt(s3, "e2", [EH2 + 1, NE, 4 * P])
            WskT = sbt(s3, "WskT", [P, KD, D])
            W1T = sbt(s3, "W1T", [P, KD, HID])
            W2T = sbt(s3, "W2T", [P, KH, D])
            sW1 = sbt(s3, "sW1", [P, KD, D])
            sW2 = sbt(s3, "sW2", [P, KD, P])
            sW3 = sbt(s3, "sW3", [P, D])
            eW1 = sbt(s3, "eW1", [P, KD, NE, P])
            eW2 = sbt(s3, "eW2", [P, NE, EH2])
            eW3 = sbt(s3, "eW3", [EH2 + 1, NE, D])
            gW = sbt(s3, "gW", [P, KD, NE])
            rows = sbt(s3, "rows", [P, 3 * D + NE])
            b1c = sbt(s3, "b1c", [P, KH])
            sb1c = sbt(s3, "sb1c", [P, KD])
            sb2c = sbt(s3, "sb2c", [P, 1])
            eb1c = sbt(s3, "eb1c", [P, NE])
            eb2c = sbt(s3, "eb2c", [EH2, NE])
            lnp = sbt(s3, "lnp", [P, 4, D])
            wbt = sbt(s3, "wbt", [P, 3, D])
            w12 = sbt(s3, "w12", [P, D])
            w23 = sbt(s3, "w23", [P, D])
            eps3 = sbt(s3, "eps3", [P, 1])
            tri = sbt(s3, "tri", [P, NE, NE])
            rl = sbt(s3, "rl", [P, W * H])
            st3 = sbt(s3, "st3", [P, W, 6])
            mn3 = sbt(s3, "mn3", [P, W])
            vr3 = sbt(s3, "vr3", [P, W])
            lv3 = sbt(s3, "lv3", [P, W])
            rs3 = sbt(s3, "rs3", [P, W])
            zb = sbt(s3, "zb", [P, W])
            ezb = sbt(s3, "ezb", [P, W])
            g4 = sbt(s3, "g4", [P, W, NE])
            gx = sbt(s3, "gx", [P, W, NE])
            gs = sbt(s3, "gs", [P, W])
            c1 = sbt(s3, "c1", [P, W, NE, NE])
            c2 = sbt(s3, "c2", [P, W, NE, NE])
            rank = sbt(s3, "rank", [P, W, NE])
            we = sbt(s3, "we", [P, W, NE])
            NATS = 3
            tr = [pst(s3, f"tr{i}", [P, 4 * P]) for i in range(2)]
            hid = [pst(s3, f"hid{i}", [P, 4 * P]) for i in range(2)]
            nat = [pst(s3, f"nat{i}", [P, 4 * P]) for i in range(NATS)]
            pg = pst(s3, "pg", [P, 4 * P])

            parts = [(t0, min(t0 + 4, W)) for t0 in range(0, W, 4)]
            NPT = len(parts)
            assert NPT <= 2
            HIDN = NPT * (KH + KD + 1 + 2 * NE)
            NATN = W * (3 + NE)
            ws_landed, w3_landed, consts3, rows_set = sem("ws_landed"), sem("w3_landed"), sem("consts3"), sem("rows_set")
            xn_landed, xb_landed, xn_used, x_used, out_ready, out_stored, out_free = (
                sem("xn_landed3"), sem("xb_landed3"), sem("xn_used3"), sem("x_used3"), sem("out_ready"), sem("out_stored"), sem("out_free"))
            tr_filled, tr_emptied = sem("tr_f3"), sem("tr_e3")
            hid_filled, hid_emptied = sem("hid_f3"), sem("hid_e3")
            nat_filled, nat_emptied = sem("nat_f3"), sem("nat_e3")
            ob_ready = sem("ob_ready")
            z_ready, ez_ready, var_ready, rstd_ready = sem("z_ready"), sem("ez_ready"), sem("var_ready3"), sem("rstd_ready3")
            y_ready, m_ready, pg_filled, gl_ready, ge_ready = (
                sem("y_ready"), sem("m_ready"), sem("pg_filled"), sem("gl_ready"), sem("ge_ready"))
            store_turns = sem("store_turns")

            with nc.Block() as block:
                @block.sync
                def _(sp):
                    loads = [
                        (WskT[:, :, :], a["WskipT"].rearrange("(k p) c -> p k c", p=P)),
                        (rows[:, 0:D], a["bskip"].partition_broadcast(P)),
                        (rows[:, D:2 * D], a["b2"].partition_broadcast(P)),
                        (rows[:, 2 * D:3 * D], a["sb3"].partition_broadcast(P)),
                        (rows[:, 3 * D:3 * D + NE], a["gb"].partition_broadcast(P)),
                        (wbt[:, :, :], a["Wbeta"].rearrange("(k d) -> k d", k=3).partition_broadcast(P)),
                        (lnp[:, 0, :], a["ln1_g"].partition_broadcast(P)),
                        (lnp[:, 1, :], a["ln1_b"].partition_broadcast(P)),
                        (lnp[:, 2, :], a["ln2_g"].partition_broadcast(P)),
                        (lnp[:, 3, :], a["ln2_b"].partition_broadcast(P)),
                        (W1T[:, :, :], a["W1T"].rearrange("(k p) c -> p k c", p=P)),
                        (W2T[:, :, :], a["W2T"].rearrange("(k p) c -> p k c", p=P)),
                        (b1c[:, :], a["b1"]),
                        (sW1[:, :, :], a["sW1"].rearrange("(k p) c -> p k c", p=P)),
                        (sW2[:, :, :], a["sW2"].rearrange("(k p) c -> p k c", p=P)),
                        (sW3[:, :], a["sW3"]),
                        (sb1c[:, :], a["sb1"]),
                        (sb2c[:, :], a["sb2"].rearrange("(p o) -> p o", o=1)),
                        (eb1c[:, :], a["eb1"]),
                        (eb2c[:, :], a["eb2"]),
                        (eW3[EH2:EH2 + 1, :, :], a["eb3"].rearrange("(a e) d -> a e d", a=1)),
                        (eW2[:, :, :], a["eW2"].rearrange("e p c -> p e c")),
                        (eW3[0:EH2, :, :], a["eW3"].rearrange("e p c -> p e c")),
                        (gW[:, :, :], a["gW"].rearrange("(k p) e -> p k e", p=P)),
                    ] + [(eW1[:, k, :, :], a["eW1"][:, k * P:(k + 1) * P, :].rearrange("e p c -> p e c")) for k in range(KD)]
                    assert len(loads) == NW3
                    for dst, src in loads[:NW3S]:
                        sp.dma_start(dst, src).then_inc(ws_landed, 16)
                    sp.dma_start(xnb[:, :, :], xn_v[:, 0:W, :]).then_inc(xn_landed, 16)
                    for dst, src in loads[NW3S:]:
                        sp.dma_start(dst, src).then_inc(w3_landed, 16)
                    sp.dma_start(xb[:, :, :], x_d[:, 0:W, :]).then_inc(xb_landed, 16)
                    if N7 > 1:
                        with sp.Fori(1, N7) as i:
                            sp.wait_ge(xn_used, i)
                            sp.dma_start(xnb[:, :, :], xn_v[:, bass.ds(i * W, W), :]).then_inc(xn_landed, 16)
                            sp.wait_ge(x_used, i)
                            sp.dma_start(xb[:, :, :], x_d[:, bass.ds(i * W, W), :]).then_inc(xb_landed, 16)

                @block.gpsimd
                def _(pool):
                    pool.memset(tri[:, :, :], 1.0).then_inc(consts3, 1)
                    pool.wait_ge(consts3, 1)
                    pool.affine_select(out=tri[:, :, :], in_=tri[:, :, :], compare_op=ALU.is_ge, fill=0.0, base=-1,
                                       pattern=[[1, NE], [-1, NE]], channel_multiplier=0).then_inc(consts3, 1)
                    pool.sem_inc(out_free, 1)
                    if N7 > 1:
                        with pool.Fori(0, N7 - 1) as i:
                            pool.wait_ge(out_ready, i + 1)
                            pool.sem_inc(store_turns, 1)
                            pool.dma_start(out[bass.ds(i * W * P, W * P), :].rearrange("(j p) d -> p j d", p=P), accb[:, :, :]
                                           ).then_inc(out_stored, 16)
                            pool.wait_ge(out_stored, i * 16 + 16)
                            pool.sem_inc(out_free, 1)
                    pool.wait_ge(out_ready, N7)
                    r0 = (N7 - 1) * W * P
                    whole = (N - r0) // P
                    last = N - r0 - whole * P
                    if whole:
                        pool.dma_start(out[r0:r0 + whole * P, :].rearrange("(j p) d -> p j d", p=P), accb[:, 0:whole, :]
                                       ).then_inc(out_stored, 16)
                    if last:
                        pool.dma_start(out[r0 + whole * P:N, :], accb[0:last, whole, :]).then_inc(out_stored, 16)
                    pool.wait_ge(out_stored, 16 * (N7 - 1 + (whole > 0) + (last > 0)))

                @block.vector
                def _(dve):
                    ch = Chain(dve, "dve3")
                    dve.sem_inc(nat_emptied, 1)
                    dve.memset(eps3[:, :], LN_EPS).then_inc(rows_set, 1)
                    dve.memset(e2[EH2:EH2 + 1, :, :], 1.0).then_inc(rows_set, 1)
                    dve.wait_ge(ws_landed, 16 * NW3S)
                    dve.wait_ge(consts3, 2)
                    ch.step(dve.tensor_add(w12[:, :], wbt[:, 0, :], wbt[:, 1, :]))
                    ch.step(dve.tensor_sub(w23[:, :], wbt[:, 1, :], wbt[:, 2, :]))
                    base = ch.n
                    with dve.Fori(0, N7) as i:
                        ch.base, ch.n = dve.snap(i * (DVE3 * NPT + DVE3_STEP) + base), 0
                        nat_i = dve.snap(i * NATN)
                        lns = [0]

                        def wide(v, w):
                            return v[:, None, :].to_broadcast([P, w, D])

                        def layernorm(dst, src, t0, t1):
                            for j in range(t0, t1):
                                s = dve.bn_stats(st3[:, j, :], src[:, j, :])
                            ch.step(s)
                            mean_and_var(dve, ch, st3[:, t0:t1, :], mn3[:, t0:t1], vr3[:, t0:t1], D)
                            dve.sem_inc(var_ready, 1)
                            lns[0] += 1
                            dve.wait_ge(rstd_ready, i * (6 * NPT) + 2 * lns[0])
                            for j in range(t0, t1):
                                s = dve.tensor_scalar(dst[:, j, :], src[:, j, :], mn3[:, j:j + 1], rs3[:, j:j + 1],
                                                      ALU.subtract, ALU.mult)
                            return s

                        def after_attention(p, t0, t1):
                            w, tt = t1 - t0, slice(t0, t1)
                            ch.step(dve.tensor_tensor(yb[:, tt, :], db[:, tt, :], wide(w23, w), ALU.mult))
                            ch.step(dve.tensor_add(tb[:, tt, :], tb[:, tt, :], yb[:, tt, :]))
                            dve.tensor_reduce(zb[:, tt], tb[:, tt, :], AX.X, ALU.add).then_inc(z_ready, 1)
                            dve.wait_ge(ez_ready, i * NPT + (p + 1))
                            ch.step(dve.tensor_scalar(ezb[:, tt], ezb[:, tt], 1.0, None, ALU.add))
                            ch.step(dve.reciprocal(ezb[:, tt], ezb[:, tt]))
                            for j in range(t0, t1):
                                s = dve.scalar_tensor_tensor(out=tb[:, j, :], in0=db[:, j, :], scalar=ezb[:, j:j + 1],
                                                             in1=ob[:, j, :], op0=ALU.mult, op1=ALU.add)
                            ch.step(s)
                            dve.wait_ge(xn_landed, i * 16 + 16)
                            ch.step(dve.tensor_add(tb[:, tt, :], tb[:, tt, :], xnb[:, tt, :]))
                            if p == NPT - 1:
                                dve.sem_inc(xn_used, 1)
                            ch.step(layernorm(db, tb, t0, t1))
                            ch.step(dve.tensor_tensor(db[:, tt, :], db[:, tt, :], wide(lnp[:, 0, :], w), ALU.mult))
                            dve.tensor_tensor(yb[:, tt, :], db[:, tt, :], wide(lnp[:, 1, :], w), ALU.add).then_inc(y_ready, 1)
                            dve.wait_ge(y_ready, i * NPT + (p + 1))
                            ch.step(dve.tensor_tensor(db[:, tt, :], yb[:, tt, :], wide(rows[:, D:2 * D], w), ALU.add))

                        def after_ffn(p, t0, t1):
                            w, tt = t1 - t0, slice(t0, t1)
                            for j in range(t0, t1):
                                n = W + j
                                dve.wait_ge(nat_filled, nat_i + (n + 1))
                                dve.tensor_add(tb[:, j, :], nat[n % NATS][:, 0:D], db[:, j, :]).then_inc(nat_emptied, 1)
                            dve.wait_ge(nat_emptied, nat_i + (W + t1 + 1))
                            ch.step(layernorm(db, tb, t0, t1))
                            ch.step(dve.tensor_tensor(db[:, tt, :], db[:, tt, :], wide(lnp[:, 2, :], w), ALU.mult))
                            ch.step(dve.tensor_tensor(db[:, tt, :], db[:, tt, :], wide(lnp[:, 3, :], w), ALU.add))
                            dve.wait_ge(xb_landed, i * 16 + 16)
                            ch.step(dve.tensor_add(tb[:, tt, :], db[:, tt, :], xb[:, tt, :]))
                            if p == NPT - 1:
                                dve.sem_inc(x_used, 1)
                            layernorm(yb, tb, t0, t1).then_inc(m_ready, 1)
                            dve.wait_ge(m_ready, i * NPT + (p + 1))
                            ch.step(dve.tensor_tensor(tb[:, tt, :], tb[:, tt, :], wide(rows[:, 2 * D:3 * D], w), ALU.add))

                        def gates(p, t0, t1):
                            w, tt = t1 - t0, slice(t0, t1)
                            dve.wait_ge(pg_filled, i * NPT + (p + 1))
                            lg = g4[:, tt, :]
                            ch.step(dve.tensor_tensor(lg, pg[:, t0 * NE:t1 * NE].rearrange("p (w e) -> p w e", e=NE),
                                                      rows[:, 3 * D:][:, None, :].to_broadcast([P, w, NE]), ALU.add))
                            four = lambda v: v[:, tt][:, :, None].to_broadcast([P, w, NE])
                            ch.step(dve.tensor_reduce(gs[:, tt], lg, AX.X, ALU.max))
                            dve.tensor_tensor(g4[:, tt, :], lg, four(gs), ALU.subtract).then_inc(gl_ready, 1)
                            dve.wait_ge(ge_ready, i * (2 * NPT) + (2 * p + 1))
                            ch.step(dve.tensor_reduce(gs[:, tt], gx[:, tt, :], AX.X, ALU.add))
                            ch.step(dve.reciprocal(gs[:, tt], gs[:, tt]))
                            ch.step(dve.tensor_tensor(g4[:, tt, :], gx[:, tt, :], four(gs), ALU.mult))
                            gj = g4[:, tt, None, :].to_broadcast([P, w, NE, NE])
                            ge = g4[:, tt, :, None].to_broadcast([P, w, NE, NE])
                            tr4 = tri[:, None, :, :].to_broadcast([P, w, NE, NE])
                            a1, a2 = c1[:, tt, :, :], c2[:, tt, :, :]
                            ch.step(dve.tensor_tensor(a1, gj, ge, ALU.is_gt))
                            ch.step(dve.tensor_tensor(a2, gj, ge, ALU.is_equal))
                            ch.step(dve.tensor_tensor(a2, a2, tr4, ALU.mult))
                            ch.step(dve.tensor_tensor(a1, a1, a2, ALU.add))
                            ch.step(dve.tensor_reduce(rank[:, tt, :], a1, AX.X, ALU.add))
                            ch.step(dve.tensor_scalar(rank[:, tt, :], rank[:, tt, :], 1.5, None, ALU.is_lt))
                            ch.step(dve.tensor_reduce(gs[:, tt], g4[:, tt, :], AX.X, ALU.max))
                            dve.tensor_tensor(g4[:, tt, :], g4[:, tt, :], four(gs), ALU.subtract).then_inc(gl_ready, 1)
                            dve.wait_ge(ge_ready, i * (2 * NPT) + (2 * p + 2))
                            ch.step(dve.tensor_tensor(we[:, tt, :], gx[:, tt, :], rank[:, tt, :], ALU.mult))
                            ch.step(dve.tensor_reduce(gs[:, tt], we[:, tt, :], AX.X, ALU.add))
                            ch.step(dve.reciprocal(gs[:, tt], gs[:, tt]))
                            ch.step(dve.tensor_tensor(we[:, tt, :], we[:, tt, :], four(gs), ALU.mult))

                        def combine(t0, t1):
                            for j in range(t0, t1):
                                n = 2 * W + j * (1 + NE)
                                dve.wait_ge(nat_filled, nat_i + (n + 1))
                                dve.tensor_add(accb[:, j, :], nat[n % NATS][:, 0:D], tb[:, j, :]).then_inc(nat_emptied, 1)
                                for e in range(NE):
                                    n += 1
                                    dve.wait_ge(nat_emptied, nat_i + (n + 1))
                                    dve.wait_ge(nat_filled, nat_i + (n + 1))
                                    dve.scalar_tensor_tensor(out=accb[:, j, :], in0=nat[n % NATS][:, 0:D], scalar=we[:, j, e:e + 1],
                                                             in1=accb[:, j, :], op0=ALU.mult, op1=ALU.add
                                                             ).then_inc(nat_emptied, 1)

                        Ub = U[:, bass.ds(i * W, W), :].rearrange("p a (h c) -> p (a h) c", c=CW)
                        ch.step(dve.tensor_scalar(rl[:, :], Ub[:, :, C], 1e-16, None, ALU.add))
                        ch.step(dve.reciprocal(rl[:, :], rl[:, :]))
                        dve.tensor_tensor(ob[:, :, :].rearrange("p a (h c) -> p (a h) c", c=C), Ub[:, :, 0:C],
                                          rl[:, :, None].to_broadcast([P, W * H, C]), ALU.mult).then_inc(ob_ready, 1)
                        dve.wait_ge(ob_ready, i + 1)
                        ch.step(dve.tensor_tensor(db[:, :, :], ob[:, :, :], wide(rows[:, 0:D], W), ALU.subtract))
                        ch.step(dve.tensor_tensor(tb[:, :, :], ob[:, :, :], wide(w12, W), ALU.mult))
                        for j in range(W):
                            dve.wait_ge(nat_filled, nat_i + (j + 1))
                            dve.tensor_sub(db[:, j, :], nat[j % NATS][:, 0:D], db[:, j, :]).then_inc(nat_emptied, 1)
                        dve.wait_ge(nat_emptied, nat_i + (W + 1))
                        for p, (t0, t1) in enumerate(parts):
                            after_attention(p, t0, t1)
                        for p, (t0, t1) in enumerate(parts):
                            after_ffn(p, t0, t1)
                        dve.wait_ge(out_free, i + 1)
                        for p, (t0, t1) in enumerate(parts):
                            gates(p, t0, t1)
                            combine(t0, t1)
                        dve.wait_ge(nat_emptied, nat_i + (NATN + 1))
                        dve.sem_inc(out_ready, 1)
                        assert ch.n == DVE3 * NPT + DVE3_STEP, ch.n

                @block.scalar
                def _(act):
                    act.sem_inc(tr_emptied, 1)
                    act.sem_inc(hid_emptied, 1)
                    act.wait_ge(rows_set, 2)
                    with act.Fori(0, N7) as i:
                        hid_i = act.snap(i * HIDN)
                        hn = [0]

                        def transposed(r, p):
                            for j in range(*parts[p]):
                                act.wait_ge(tr_filled, i * (3 * W) + (r * W + j + 1))
                                act.activation(rT[:, :, j * P:(j + 1) * P], tr[j % 2][:, 0:KD * P].rearrange(
                                    "p (k n) -> p k n", n=P), ACT.Copy).then_inc(tr_emptied, 1)

                        def exp_z(p):
                            tt = slice(*parts[p])
                            act.wait_ge(z_ready, i * NPT + (p + 1))
                            act.activation(ezb[:, tt], zb[:, tt], ACT.Exp, scale=-1.0).then_inc(ez_ready, 1)

                        def rstd(p):
                            tt = slice(*parts[p])
                            rn[0] += 1
                            act.wait_ge(var_ready, i * (3 * NPT) + rn[0])
                            act.activation(lv3[:, tt], vr3[:, tt], ACT.Ln, bias=eps3[:, 0:1]).then_inc(rstd_ready, 1)
                            act.wait_ge(rstd_ready, i * (6 * NPT) + (2 * rn[0] - 1))
                            act.activation(rs3[:, tt], lv3[:, tt], ACT.Exp, scale=-0.5).then_inc(rstd_ready, 1)

                        def exp_gates(p):
                            tt = slice(*parts[p])
                            en[0] += 1
                            act.wait_ge(gl_ready, i * (2 * NPT) + en[0])
                            act.activation(gx[:, tt, :], g4[:, tt, :], ACT.Exp).then_inc(ge_ready, 1)

                        def hidden(dst, func, bias, w, rws=P):
                            n = hn[0]
                            hn[0] += 1
                            act.wait_ge(hid_filled, hid_i + (n + 1))
                            act.activation(dst, hid[n % 2][0:rws, 0:w], func, bias=bias).then_inc(hid_emptied, 1)

                        rn, en = [0], [0]
                        for p in range(NPT):
                            transposed(0, p)
                        exp_z(0)
                        rstd(0)
                        transposed(1, 0)
                        act.wait_ge(w3_landed, 16 * (NW3 - NW3S))
                        for p, (t0, t1) in enumerate(parts):
                            for k in range(KH):
                                if p + 1 < NPT and k == 2:
                                    exp_z(p + 1)
                                if p + 1 < NPT and k == 6:
                                    rstd(p + 1)
                                if p >= 1 and k == 3:
                                    rstd(p - 1)
                                hidden(h1[:, k, 0:(t1 - t0) * P], ACT.Gelu, b1c[:, k:k + 1], (t1 - t0) * P)
                            if p >= 1:
                                rstd(p - 1)
                            if p + 1 < NPT:
                                transposed(1, p + 1)
                        if NPT == 1:
                            rstd(0)
                            rstd(0)
                        transposed(2, 0)
                        for p, (t0, t1) in enumerate(parts):
                            w = (t1 - t0) * P
                            for c in range(KD):
                                if p == 0 and NPT > 1 and c == 1:
                                    rstd(NPT - 1)
                                hidden(sh1[:, c, 0:w], ACT.Relu, sb1c[:, c:c + 1], w)
                            for e in range(NE):
                                if p == 0 and NPT > 1 and e == NE - 1:
                                    rstd(NPT - 1)
                                hidden(e1[:, e, 0:w], ACT.Relu, eb1c[:, e:e + 1], w)
                            hidden(sh2[:, 0:w], ACT.Relu, sb2c[:, 0:1], w)
                            for e in range(NE):
                                if e >= NE - 2:
                                    exp_gates(p)
                                hidden(e2[0:EH2, e, 0:w], ACT.Relu, eb2c[:, e:e + 1], w, EH2)
                            if p + 1 < NPT:
                                transposed(2, p + 1)
                        assert hn[0] == HIDN

                @block.tensor
                def _(pe):
                    pe.wait_ge(ws_landed, 16 * NW3S)
                    pe.wait_ge(rows_set, 2)
                    with pe.Fori(0, N7) as i:
                        hid_i = pe.snap(i * HIDN)
                        nat_i = pe.snap(i * NATN)
                        hn, nn = [0], [0]

                        def transpose_rows(r, src, p):
                            for j in range(*parts[p]):
                                pe.wait_ge(tr_emptied, i * (3 * W) + (r * W + j + (0 if j else 1)))
                                for k in range(KD):
                                    m = pe.transpose(tr[j % 2][:, k * P:(k + 1) * P], src[:, j, k * P:(k + 1) * P], ident[:, :])
                                m.then_inc(tr_filled, 1)

                        def hidden(rws, w, terms):
                            n = hn[0]
                            hn[0] += 1
                            pe.wait_ge(hid_emptied, hid_i + max(n, 1))
                            for q, (l, r) in enumerate(terms):
                                m = pe.matmul(hid[n % 2][0:rws, 0:w], l, r, start=(q == 0), stop=(q == len(terms) - 1))
                            m.then_inc(hid_filled, 1)

                        def node_major(terms):
                            n = nn[0]
                            nn[0] += 1
                            pe.wait_ge(nat_emptied, nat_i + max(n + 2 - NATS, 1))
                            for q, (l, r) in enumerate(terms):
                                m = pe.matmul(nat[n % NATS][:, 0:D], l, r, start=(q == 0), stop=(q == len(terms) - 1))
                            m.then_inc(nat_filled, 1)

                        pe.wait_ge(xn_landed, i * 16 + 16)
                        for p in range(NPT):
                            transpose_rows(0, xnb, p)
                        for j in range(W):
                            pe.wait_ge(tr_emptied, i * (3 * W) + (j + 2))
                            node_major([(rT[:, k, j * P:(j + 1) * P], WskT[:, k, :]) for k in range(KD)])
                        pe.wait_ge(w3_landed, 16 * (NW3 - NW3S))
                        for p, (t0, t1) in enumerate(parts):
                            pe.wait_ge(y_ready, i * NPT + (p + 1))
                            transpose_rows(1, yb, p)
                            w = (t1 - t0) * P
                            pe.wait_ge(tr_emptied, i * (3 * W) + (W + t1 + 1))
                            for c in range(KH):
                                hidden(P, w, [(W1T[:, k, c * P:(c + 1) * P], rT[:, k, t0 * P:t1 * P]) for k in range(KD)])
                            pe.wait_ge(hid_emptied, hid_i + (hn[0] + 1))
                            for j in range(t1 - t0):
                                node_major([(h1[:, k, j * P:(j + 1) * P], W2T[:, k, :]) for k in range(KH)])
                        for p, (t0, t1) in enumerate(parts):
                            pe.wait_ge(m_ready, i * NPT + (p + 1))
                            transpose_rows(2, yb, p)
                            pe.wait_ge(tr_emptied, i * (3 * W) + (2 * W + t1 + 1))
                            for j in range(t0, t1):
                                for k in range(KD):
                                    m = pe.matmul(pg[:, j * NE:(j + 1) * NE], rT[:, k, j * P:(j + 1) * P], gW[:, k, :],
                                                  start=(k == 0), stop=(k == KD - 1))
                            m.then_inc(pg_filled, 1)
                            w = (t1 - t0) * P
                            for c in range(KD):
                                hidden(P, w, [(sW1[:, k, c * P:(c + 1) * P], rT[:, k, t0 * P:t1 * P]) for k in range(KD)])
                            for e in range(NE):
                                hidden(P, w, [(eW1[:, k, e, :], rT[:, k, t0 * P:t1 * P]) for k in range(KD)])
                            pe.wait_ge(hid_emptied, hid_i + (hn[0] - NE + 1))
                            hidden(P, w, [(sW2[:, k, :], sh1[:, k, 0:w]) for k in range(KD)])
                            for e in range(NE):
                                pe.wait_ge(hid_emptied, hid_i + (hn[0] - 1 - e - (NE - 1 - e) + 1))
                                hidden(EH2, w, [(eW2[:, e, :], e1[:, e, 0:w])])
                            pe.wait_ge(hid_emptied, hid_i + (hn[0] + 1))
                            for j in range(t1 - t0):
                                cols = slice(j * P, (j + 1) * P)
                                node_major([(sh2[:, cols], sW3[:, :])])
                                for e in range(NE):
                                    node_major([(e2[:, e, cols], eW3[:, e, :])])
                        assert (hn[0], nn[0]) == (HIDN, NATN)


NW3, NW3S = 26, 10
DVE3, DVE3_STEP = 54, 4


def kernel(**inputs):
    import concourse.bacc as _bacc
    from concourse.bass_utils import run_bass_kernel_spmd as _run

    g = {k: np.asarray(v) for k, v in inputs.items()}
    N, D = g["x"].shape
    E, DE = g["edge_attr_64"].shape
    NP = -(-N // P) * P
    tiles = -(-int(E * 16 * 1.1) // (N * P))
    CH = tiles * P
    EP = -(-(E + CH) // P) * P
    x = np.zeros((NP, D), np.float32)
    x[:N] = g["x"]
    src = np.zeros(EP, np.int32)
    src[:E] = g["src"]
    dst = np.full(EP, 1 << 20, np.int32)
    dst[:E] = g["dst"]
    ea = np.zeros((EP, DE), np.float32)
    ea[:E] = g["edge_attr_64"]

    def T(w):
        return np.ascontiguousarray(np.swapaxes(w, -1, -2))

    def cols(v):
        return np.ascontiguousarray(v.reshape(-1, P).T)

    arrays = {
        "x": x, "src": src, "dst": dst, "dst_first": dst[::P].copy(), "edge_attr": ea, "edge_attrT": np.ascontiguousarray(ea.T),
        "WqT": T(g["L0_gnn_Wq"]), "bq": cols(g["L0_gnn_bq"]), "Wk": g["L0_gnn_Wk"],
        "W3": np.concatenate([g["L0_gnn_We"], g["L0_gnn_bk"][:, None]], axis=1),
        "WvT": T(g["L0_gnn_Wv"]), "bv": g["L0_gnn_bv"], "WeT": T(g["L0_gnn_We"]),
        "ones": np.ones(8, np.float32), "WskipT": T(g["L0_gnn_Wskip"]), "bskip": g["L0_gnn_bskip"],
        "Wbeta": g["L0_gnn_Wbeta"].reshape(-1), "W1T": T(g["L0_gnn_W1"]), "W2T": T(g["L0_gnn_W2"]),
    }
    for n in ("ln1_g", "ln1_b", "ln2_g", "ln2_b", "b1", "b2"):
        arrays[n] = g[f"L0_gnn_{n}"]
    for n in ("sW1", "sb1", "sW2", "sb2", "sW3", "sb3", "eW1", "eb1", "eW2", "eb2", "eW3", "eb3", "gW", "gb"):
        arrays[n] = g[f"L0_ffn_{n}"]
    arrays["b1"], arrays["sb1"] = cols(arrays["b1"]), cols(arrays["sb1"])
    arrays["eb1"], arrays["eb2"] = T(arrays["eb1"]), T(arrays["eb2"])

    nc = _bacc.Bacc("TRN2", target_bir_lowering=False, num_devices=1)
    maps, aps = {}, {}
    for name, v in arrays.items():
        maps[f"in_{name}"] = np.ascontiguousarray(v)
        aps[name] = nc.dram_tensor(f"in_{name}", v.shape, mybir.dt.from_np(v.dtype), kind="ExternalInput").ap()
    aps["tiles"], aps["edges"] = tiles, E
    out = nc.dram_tensor("out_dram", (N, D), F32, kind="ExternalOutput").ap()
    with nc.allow_non_contiguous_dma(reason="a few short rows of weights"):
        build(nc, aps, out)
    r = _run(nc, [maps], core_ids=[0])
    return r.results[0]["out_dram"]
```
